# Optimizing a Trainium2 kernel written in Bass

```python
import numpy as np
import jax
import jax.numpy as jnp

def _softmax(x, axis=-1):
    return jax.nn.softmax(x, axis=axis)

def _gelu(x):
    return jax.nn.gelu(x, approximate=True)

def _silu(x):
    return jax.nn.silu(x)

def _sigmoid(x):
    return jax.nn.sigmoid(x)

def _layernorm(x, axis=-1, eps=1e-05):
    m = jnp.mean(x, axis=axis, keepdims=True)
    v = jnp.var(x, axis=axis, keepdims=True)
    return (x - m) / jnp.sqrt(v + eps)

def _scatter_add(tgt, idx, src, axis=0):
    return tgt.at[idx].add(src)

def _segment_sum(src, seg, n):
    return jax.ops.segment_sum(src, seg, n)
kernel_name = 'mk_adaln_ffn_d1_seqx_r4_cce86b'

def setup_inputs(seed: int=0):
    np.random.seed(seed)
    _w = jnp.asarray

    def _rec_inputs():
        import jax
        import jax.numpy as jnp
        _rk = jax.random.key(seed)
        x = -0.0003929 + 0.9999 * jax.random.normal(jax.random.fold_in(_rk, 1), (64, 64, 256), jnp.float32)
        _lenS = 64 - jax.random.randint(jax.random.fold_in(_rk, 7), (64,), 0, max(1, 64 // 4) + 1, jnp.int32)
        _lenS2 = 64 - jax.random.randint(jax.random.fold_in(_rk, 8), (64,), 0, max(1, 64 // 4) + 1, jnp.int32)
        cond_2048 = 0.00782532 + 1.00527 * jax.random.normal(jax.random.fold_in(_rk, 11), (64, 512), jnp.float32)
        return (x, cond_2048)
    x, cond_2048 = _rec_inputs()

    def _L0_cond_setup():
        import jax, jax.numpy as jnp
        import numpy as np
        B, S, D_MODEL, D_INNER, D_STATE = (4, 1024, 256, 512, 16)
        key = jax.random.key(seed)
        ks = jax.random.split(key, 12)
        inp = {'x': jax.random.normal(ks[0], (B, S, D_MODEL), jnp.float32), 't_emb': jax.random.normal(ks[1], (B, D_INNER), jnp.float32), 'W_in': jax.random.normal(ks[2], (2 * D_INNER, D_MODEL), jnp.float32) * 0.02, 'W_conv': jax.random.normal(ks[3], (D_INNER, 1, 4), jnp.float32) * 0.1, 'b_conv': jnp.zeros((D_INNER,), jnp.float32), 'ln_g': jnp.ones((D_INNER,), jnp.float32), 'ln_b': jnp.zeros((D_INNER,), jnp.float32), 'W_xproj': jax.random.normal(ks[4], (3 * D_STATE, D_INNER), jnp.float32) * 0.02, 'W_dt': jax.random.normal(ks[5], (D_STATE, D_STATE), jnp.float32) * 0.01, 'b_dt': jax.random.uniform(ks[6], (D_STATE,), jnp.float32) * 0.1, 'A_log': jax.random.normal(ks[7], (D_STATE,), jnp.float32) * 0.1, 'D': jnp.ones((D_INNER,), jnp.float32) * 0.1, 'W_out': jax.random.normal(ks[8], (D_MODEL, D_INNER), jnp.float32) * 0.02}
        return inp
    _L0_cond_all = _L0_cond_setup()
    _L0_cond_in = {k: v for k, v in _L0_cond_all.items() if k in ('W_in', 'W_conv', 'b_conv', 'ln_g', 'ln_b', 'W_xproj', 'W_dt', 'b_dt', 'A_log', 'D', 'W_out')}
    del _L0_cond_all

    def _L0_ffn_setup():
        import jax, jax.numpy as jnp
        import numpy as np
        DIM = 256
        HEADS = 16
        HD = DIM // HEADS
        M = 64
        E = 4
        K = 2
        HID = 512
        MID = 512
        LB = 0.01
        EPS = 1.1920929e-07

        def _rms(x, w):
            return x * jax.lax.rsqrt(jnp.mean(x * x, axis=-1, keepdims=True) + EPS) * w

        def _gelu(x):
            return jax.nn.gelu(x, approximate=False)
        key = jax.random.key(seed)
        ks = jax.random.split(key, 20)
        d = DIM
        w = lambda k, s: jax.random.normal(k, s, jnp.float32) * 0.02
        return {'x': jax.random.normal(ks[0], (4, 256, d), jnp.float32), 'n1_w': jnp.ones((d,), jnp.float32), 'n2_w': jnp.ones((d,), jnp.float32), 'wq': w(ks[1], (d, d)), 'wk': w(ks[2], (d, d)), 'wv': w(ks[3], (d, d)), 'wo': w(ks[4], (d, d)), 'qn_w': jnp.ones((HD,), jnp.float32), 'kn_w': jnp.ones((HD,), jnp.float32), 'gate_w': w(ks[5], (E, d)), 'e0_up': w(ks[6], (HID, d)), 'e0_down': w(ks[7], (d, HID)), 'e1_w1': w(ks[8], (HID, d)), 'e1_w2': w(ks[9], (HID, d)), 'e1_down': w(ks[10], (d, HID)), 'e2_l1': w(ks[11], (MID, d)), 'e2_l2': w(ks[12], (HID, MID)), 'e2_l3': w(ks[13], (MID, HID)), 'e2_l4': w(ks[14], (d, MID)), 'e3_down': w(ks[15], (d, d)), 'e3_up': w(ks[16], (HID, d)), 'e3_out': w(ks[17], (d, HID))}
    _L0_ffn_all = _L0_ffn_setup()
    _L0_ffn_in = {k: v for k, v in _L0_ffn_all.items() if k in ('n1_w', 'n2_w', 'wq', 'wk', 'wv', 'wo', 'qn_w', 'kn_w', 'gate_w', 'e0_up', 'e0_down', 'e1_w1', 'e1_w2', 'e1_down', 'e2_l1', 'e2_l2', 'e2_l3', 'e2_l4', 'e3_down', 'e3_up', 'e3_out')}
    del _L0_ffn_all
    return {'x': x, 'cond_2048': cond_2048, 'L0_cond_W_in': _L0_cond_in['W_in'], 'L0_cond_W_conv': _L0_cond_in['W_conv'], 'L0_cond_b_conv': _L0_cond_in['b_conv'], 'L0_cond_ln_g': _L0_cond_in['ln_g'], 'L0_cond_ln_b': _L0_cond_in['ln_b'], 'L0_cond_W_xproj': _L0_cond_in['W_xproj'], 'L0_cond_W_dt': _L0_cond_in['W_dt'], 'L0_cond_b_dt': _L0_cond_in['b_dt'], 'L0_cond_A_log': _L0_cond_in['A_log'], 'L0_cond_D': _L0_cond_in['D'], 'L0_cond_W_out': _L0_cond_in['W_out'], 'L0_ffn_n1_w': _L0_ffn_in['n1_w'], 'L0_ffn_n2_w': _L0_ffn_in['n2_w'], 'L0_ffn_wq': _L0_ffn_in['wq'], 'L0_ffn_wk': _L0_ffn_in['wk'], 'L0_ffn_wv': _L0_ffn_in['wv'], 'L0_ffn_wo': _L0_ffn_in['wo'], 'L0_ffn_qn_w': _L0_ffn_in['qn_w'], 'L0_ffn_kn_w': _L0_ffn_in['kn_w'], 'L0_ffn_gate_w': _L0_ffn_in['gate_w'], 'L0_ffn_e0_up': _L0_ffn_in['e0_up'], 'L0_ffn_e0_down': _L0_ffn_in['e0_down'], 'L0_ffn_e1_w1': _L0_ffn_in['e1_w1'], 'L0_ffn_e1_w2': _L0_ffn_in['e1_w2'], 'L0_ffn_e1_down': _L0_ffn_in['e1_down'], 'L0_ffn_e2_l1': _L0_ffn_in['e2_l1'], 'L0_ffn_e2_l2': _L0_ffn_in['e2_l2'], 'L0_ffn_e2_l3': _L0_ffn_in['e2_l3'], 'L0_ffn_e2_l4': _L0_ffn_in['e2_l4'], 'L0_ffn_e3_down': _L0_ffn_in['e3_down'], 'L0_ffn_e3_up': _L0_ffn_in['e3_up'], 'L0_ffn_e3_out': _L0_ffn_in['e3_out']}

def reference(x, cond_2048, L0_cond_W_in, L0_cond_W_conv, L0_cond_b_conv, L0_cond_ln_g, L0_cond_ln_b, L0_cond_W_xproj, L0_cond_W_dt, L0_cond_b_dt, L0_cond_A_log, L0_cond_D, L0_cond_W_out, L0_ffn_n1_w, L0_ffn_n2_w, L0_ffn_wq, L0_ffn_wk, L0_ffn_wv, L0_ffn_wo, L0_ffn_qn_w, L0_ffn_kn_w, L0_ffn_gate_w, L0_ffn_e0_up, L0_ffn_e0_down, L0_ffn_e1_w1, L0_ffn_e1_w2, L0_ffn_e1_down, L0_ffn_e2_l1, L0_ffn_e2_l2, L0_ffn_e2_l3, L0_ffn_e2_l4, L0_ffn_e3_down, L0_ffn_e3_up, L0_ffn_e3_out):
    import jax
    import jax.numpy as jnp

    def _L0_cond_ref(x, t_emb, W_in, W_conv, b_conv, ln_g, ln_b, W_xproj, W_dt, b_dt, A_log, D, W_out):
        import jax, jax.numpy as jnp
        import numpy as np
        B, S, D_MODEL, D_INNER, D_STATE = (4, 1024, 256, 512, 16)
        d_inner = W_conv.shape[0]
        d_state = A_log.shape[0]
        xr, gate = jnp.split(x @ W_in.T, 2, axis=-1)
        xr = xr + t_emb[:, None, :]
        xc = jax.lax.conv_general_dilated(xr.transpose(0, 2, 1), W_conv, (1,), [(3, 0)], feature_group_count=d_inner, dimension_numbers=('NCH', 'OIH', 'NCH')) + b_conv[None, :, None]
        xc = jax.nn.silu(xc).transpose(0, 2, 1)
        mu = xc.mean(-1, keepdims=True)
        var = xc.var(-1, keepdims=True)
        xn = (xc - mu) / jnp.sqrt(var + 1e-05) * ln_g + ln_b
        Bm, Cm, dt = jnp.split(xn @ W_xproj.T, 3, axis=-1)
        dt = jnp.tanh(dt @ W_dt.T + b_dt) * 0.01
        A = -jnp.tanh(A_log)
        Ad = 1.0 + dt * A
        Bd = Bm * jnp.minimum(jnp.linalg.norm(xn, axis=-1, keepdims=True), 1.0)
        h0 = jnp.zeros((xn.shape[0], d_state, d_inner), xn.dtype)

        def step(h, inputs):
            ad, bd, xt, ct = inputs
            h = jnp.clip(h * ad[:, :, None] + bd[:, :, None] * xt[:, None, :], -10.0, 10.0)
            yt = jnp.einsum('bd,bdh->bh', ct, h)
            return (h, yt)
        _, ys = jax.lax.scan(step, h0, (Ad.transpose(1, 0, 2), Bd.transpose(1, 0, 2), xn.transpose(1, 0, 2), Cm.transpose(1, 0, 2)))
        y = ys.transpose(1, 0, 2) + D * xn
        return y * jax.nn.silu(gate) @ W_out.T

    def _L0_ffn_ref(x, n1_w, n2_w, wq, wk, wv, wo, qn_w, kn_w, gate_w, e0_up, e0_down, e1_w1, e1_w2, e1_down, e2_l1, e2_l2, e2_l3, e2_l4, e3_down, e3_up, e3_out):
        import jax, jax.numpy as jnp
        import numpy as np
        DIM = 256
        HEADS = 16
        HD = DIM // HEADS
        M = 64
        E = 4
        K = 2
        HID = 512
        MID = 512
        LB = 0.01
        EPS = 1.1920929e-07

        def _rms(x, w):
            return x * jax.lax.rsqrt(jnp.mean(x * x, axis=-1, keepdims=True) + EPS) * w

        def _gelu(x):
            return jax.nn.gelu(x, approximate=False)
        B, T, C = x.shape
        h = _rms(x, n1_w)
        heads = lambda w_: (h @ w_.T).reshape(B, T, HEADS, HD).transpose(0, 2, 1, 3)
        q = _rms(heads(wq), qn_w)
        k = _rms(heads(wk), kn_w)
        v = heads(wv)
        scores = jnp.einsum('bhqd,bhkd->bhqk', q, k) * HD ** (-0.5)
        causal = jnp.tril(jnp.ones((T, T), bool))
        scores = jnp.where(causal[None, None], scores, -jnp.inf)
        attn = jax.nn.softmax(scores, axis=-1)
        ao = jnp.einsum('bhqk,bhkd->bhqd', attn, v).transpose(0, 2, 1, 3).reshape(B, T, C) @ wo.T
        ao = ao.at[:, :, :M].set(0.0)
        x = x + ao
        xf = _rms(x, n2_w).reshape(-1, C)
        N = xf.shape[0]
        logits = jnp.nan_to_num(xf @ gate_w.T)
        probs = jax.nn.softmax(logits, axis=-1)
        topv, topi = jax.lax.top_k(probs, K)
        topv = topv / (topv.sum(-1, keepdims=True) + 1e-08)
        wts = jnp.zeros((N, E), x.dtype).at[jnp.arange(N)[:, None], topi].add(topv)
        o0 = _gelu(xf @ e0_up.T) @ e0_down.T
        o1 = jax.nn.silu(xf @ e1_w1.T) * (xf @ e1_w2.T) @ e1_down.T
        o2 = _gelu(_gelu(_gelu(xf @ e2_l1.T) @ e2_l2.T) @ e2_l3.T) @ e2_l4.T
        o3 = _gelu(_gelu(xf @ e3_down.T) @ e3_up.T) @ e3_out.T
        moe = wts[:, 0:1] * o0 + wts[:, 1:2] * o1 + wts[:, 2:3] * o2 + wts[:, 3:4] * o3
        moe = moe.reshape(B, T, C).at[:, :, :M].set(0.0)
        return x + moe
    x = x + _L0_ffn_ref(_L0_cond_ref(x, cond_2048, L0_cond_W_in, L0_cond_W_conv, L0_cond_b_conv, L0_cond_ln_g, L0_cond_ln_b, L0_cond_W_xproj, L0_cond_W_dt, L0_cond_b_dt, L0_cond_A_log, L0_cond_D, L0_cond_W_out), L0_ffn_n1_w, L0_ffn_n2_w, L0_ffn_wq, L0_ffn_wk, L0_ffn_wv, L0_ffn_wo, L0_ffn_qn_w, L0_ffn_kn_w, L0_ffn_gate_w, L0_ffn_e0_up, L0_ffn_e0_down, L0_ffn_e1_w1, L0_ffn_e1_w2, L0_ffn_e1_down, L0_ffn_e2_l1, L0_ffn_e2_l2, L0_ffn_e2_l3, L0_ffn_e2_l4, L0_ffn_e3_down, L0_ffn_e3_up, L0_ffn_e3_out)
    return x

_drawn_inputs = setup_inputs


def setup_inputs(seed=0):
    import zlib

    import numpy as np

    out = dict(_drawn_inputs(seed))
    spreads = {'L0_cond_b_conv': (0.0, 0.1),
     'L0_cond_ln_g': (1.0, 0.2),
     'L0_cond_ln_b': (0.0, 0.1),
     'L0_cond_D': (0.10000000149011612, 0.6),
     'L0_ffn_n1_w': (1.0, 0.6),
     'L0_ffn_n2_w': (1.0, 0.6),
     'L0_ffn_qn_w': (1.0, 0.6),
     'L0_ffn_kn_w': (1.0, 0.6)}
    factors = {'L0_cond_W_dt': 8.0,
     'L0_cond_b_dt': 8.0,
     'L0_cond_A_log': 8.0,
     'L0_ffn_wq': 2.763,
     'L0_ffn_wk': 2.724,
     'L0_ffn_gate_w': 3.455,
     'L0_ffn_e0_up': 10.537,
     'L0_ffn_e0_down': 9.174,
     'L0_ffn_e1_w1': 8.0,
     'L0_ffn_e1_w2': 8.0,
     'L0_ffn_e1_down': 8.0,
     'L0_ffn_e2_l1': 8.0,
     'L0_ffn_e2_l2': 8.0,
     'L0_ffn_e2_l3': 8.0,
     'L0_ffn_e2_l4': 8.0,
     'L0_ffn_e3_down': 8.0,
     'L0_ffn_e3_up': 8.0,
     'L0_ffn_e3_out': 8.0}
    for name, (base, spread) in spreads.items():
        noise = np.random.default_rng([zlib.crc32(name.encode()), seed]).standard_normal(out[name].shape)
        drawn = base * np.exp(spread * noise) if base else spread * noise
        out[name] = jnp.asarray(drawn.astype(out[name].dtype))
    for name, factor in factors.items():
        out[name] = (out[name] * factor).astype(out[name].dtype)
    return out
```

```python
from contextlib import ExitStack

import numpy as np

import concourse.bass as bass
from concourse import mybir

F32 = mybir.dt.float32
F32R = mybir.dt.float32r
ACT = mybir.ActivationFunctionType
ALU = mybir.AluOpType
AX = mybir.AxisListType.X

P = 128
B, T, C = 64, 64, 256
DI = 512
NS = 16
GROUPS = 8
GB = B // GROUPS
TOK = GB * T
KC, IC = C // P, DI // P
BLK = TOK // P
HEADS, HD = 16, 16
EXPERTS, TOPK = 4, 2
KEPT = 64
MOD = C - KEPT
STEPS_X = 4
NX = T // STEPS_X
RING_H = 6
CLIP = 10.0
EPS_LN, EPS_RMS, EPS_TOP = 1e-5, 1.1920929e-07, 1e-8
MASKED = -1.0e30
FMAX = 3.4028234663852886e38
NCONV = 4

W_SHAPES = {
    "w_in": (KC, 2 * DI), "w_xb": (IC, NS), "w_xcd": (IC, 48), "w_out": (IC, C),
    "w_qk": (KC, 2 * C), "w_v": (KC, C), "w_o": (KC, C), "w_gate": (KC, EXPERTS),
    "e0_up": (KC, DI), "e0_down": (IC, MOD),
    "e1_w1": (KC, DI), "e1_w2": (KC, DI), "e1_down": (IC, MOD),
    "e2_l1": (KC, DI), "e2_l2": (IC, DI), "e2_l3": (IC, DI), "e2_l4": (IC, MOD),
    "e3_down": (KC, C), "e3_up": (KC, DI), "e3_out": (IC, MOD),
    "temb": (IC, B), "w_conv": (IC, NCONV), "vecs": (4, IC), "norms": (KC, 2), "qkn": (2,),
    "dt_w": (NS + 2,),
    "ident": (P,), "sel": (BLK, P), "mean_mat": (P,), "cols": (5,), "wu_mask": (32,),
    "c_mask": (GB,), "causal": (T,), "head_mask": (8,), "rank": (2, EXPERTS * EXPERTS),
}
LOADS = [("w_in", "temb"), ("w_conv", "vecs", "mean_mat", "cols", "ident"),
         ("w_xb", "w_xcd", "dt_w", "sel", "wu_mask", "c_mask"),
         ("w_out", "norms", "w_qk", "w_v", "qkn", "head_mask", "causal", "w_o", "w_gate", "rank"),
         ("e1_w1", "e1_w2", "e1_down"), ("e0_up", "e0_down"), ("e2_l1", "e2_l2", "e2_l3", "e2_l4"),
         ("e3_down", "e3_up", "e3_out")]


class Lane:

    def __init__(self, name, engine, new_sem):
        self.name, self.engine, self.new_sem, self.counts, self.seen = name, engine, new_sem, {}, {}
        self.phase("setup")

    def phase(self, stage):
        self.key = f"{self.name}_{stage}"

    def wait(self, *after):
        for sem, value in flat(after):
            if self.seen.get(id(sem), 0) < value:
                self.engine.wait_ge(sem, value)
                self.seen[id(sem)] = value

    def do(self, build, *after):
        self.wait(after)
        n = self.counts[self.key] = self.counts.get(self.key, 0) + 1
        sem = self.new_sem(self.key)
        build(self.engine).then_inc(sem, 1)
        return sem, n

    def dma(self, sem, build, *after):
        self.wait(after)
        build(self.engine).then_inc(sem, 16)


def flat(ticks):
    if ticks is None:
        return []
    if isinstance(ticks, tuple) and len(ticks) == 2 and isinstance(ticks[1], int):
        return [ticks]
    return [t for part in ticks for t in flat(part)]


class Slots:

    def __init__(self, bufs):
        self.bufs = [(b, []) for b in bufs]

    def take(self):
        assert self.bufs, "no buffer is free"
        return self.bufs.pop(0)

    def give(self, buf, *last_readers):
        self.bufs.append((buf, flat(last_readers)))


def build_program(nc, dram, out):
    ctx = ExitStack()
    with ctx:
        def sb(name, shape, dt=F32):
            return ctx.enter_context(nc.sbuf_tensor(name, list(shape), dt))

        sems = {}

        def sem(name):
            if name not in sems:
                sems[name] = ctx.enter_context(nc.semaphore(name))
            return sems[name]

        pe, act, dve, pool, sp = (Lane(n, e, sem) for n, e in (
            ("pe", nc.tensor), ("act", nc.scalar), ("dve", nc.vector), ("pool", nc.gpsimd), ("sp", nc.sync)))
        lanes = (pe, act, dve, pool)

        def advance(stage, steps):
            for lane in lanes:
                lane.phase(stage)
            return next(steps, "end") != "end"

        w = {k: sb(k, (P,) + s) for k, s in W_SHAPES.items()}
        loaded = {}
        for n, batch in enumerate(LOADS):
            s = sem(f"weights{n}")
            for k in batch:
                sp.dma(s, lambda e, k=k: e.dma_start(w[k][:], dram[k]))
                loaded[k] = (s, 16 * len(batch))

        def ld(*names):
            return [loaded[n] for n in names]

        ident, cols = w["ident"], w["cols"]
        col_ln, col_rms, col_one = cols[:, 0:1], cols[:, 1:2], cols[:, 2:3]
        neg_half, half = cols[:, 3:4], cols[:, 4:5]
        ident_r = sb("ident_r", (P, P), F32R)
        na = sb("na", (P, 2))

        xn = [sb(f"xn{i}", (P, IC, TOK)) for i in range(4)]
        xn_free = [[] for _ in range(4)]
        ad = [sb(f"ad{i}", (P, T)) for i in range(4)]
        cc = [sb(f"cc{i}", (P, T)) for i in range(4)]
        b4 = [sb(f"b4{i}", (P, NX, NS)) for i in range(4)]
        coef_free = [[] for _ in range(4)]
        ready = [None] * GROUPS
        xr_pad = [sb(f"xr_pad{i}", (P, (T + NCONV - 1) * GB)) for i in range(2)]
        xr_slots = Slots(xr_pad)
        tiles = Slots([sb(f"tile{i}", (P, 512)) for i in range(11)])
        small = Slots([sb(f"small{i}", (P, 64)) for i in range(10)])
        vbd = Slots([sb("vbd", (P, 2, 8, 2, HD))])
        cd_pack = sb("cd_pack", (48, GB, T))
        cd_free = [[]]

        xq = sb("xq", (P, IC, 2, 2, 32), F32R)
        xrow = [[sb(f"xrow{c}{i}", (P, DI), F32R) for i in range(2)] for c in range(2)]
        wu = [[sb(f"wu{c}{i}", (P, 32, NS), F32R) for i in range(2)] for c in range(2)]
        hs = [[sb(f"h{c}{i}", (P, DI)) for i in range(RING_H)] for c in range(2)]
        pre = [sb(f"pre{c}", (P, DI)) for c in range(2)]
        ytok = sb("ytok", (P, DI))
        cdiag = [[sb(f"cdiag{c}{i}", (P, 16, 32)) for i in range(2)] for c in range(2)]

        banks = [ctx.enter_context(nc.psum_tensor(f"bank{i}", [P, 512], F32)) for i in range(8)]
        u_ps, x_ps, y_ps = banks[0:2], Slots([banks[2]]), banks[3:5]
        gen = Slots(banks[5:8])

        t_identr = dve.do(lambda e: e.tensor_copy(ident_r[:], ident[:]), ld("ident"))
        zeroed = [dve.do(lambda e, x=x: e.memset(x[:, 0:(NCONV - 1) * GB], 0.0)) for x in xr_pad]
        t_zero_cd = [dve.do(lambda e, x=x: e.memset(x[:], 0.0)) for c in cdiag for x in c]
        t_zero_v = [pool.do(lambda e, x=x: e.memset(x[:], 0.0)) for x, _ in vbd.bufs]
        t_na = act.do(lambda e: e.activation(na[32:48, 0:1], w["dt_w"][32:48, NS + 1:NS + 2], ACT.Tanh),
                      ld("dt_w"))
        t_na = dve.do(lambda e: e.tensor_scalar(na[32:48, 1:2], na[32:48, 0:1], -0.01, None, ALU.mult),
                      t_na)

        def mm(out_ap, pairs, *after):
            pairs = list(pairs)

            def go(e):
                for i, (lhs, rhs) in enumerate(pairs):
                    last = e.matmul(out_ap, lhs, rhs, start=i == 0, stop=i == len(pairs) - 1)
                return last
            return pe.do(go, *after)

        def mms(jobs, *after):
            jobs = [(o, list(ps)) for o, ps in jobs]

            def go(e):
                for o, ps in jobs:
                    for i, (lhs, rhs) in enumerate(ps):
                        last = e.matmul(o, lhs, rhs, start=i == 0, stop=i == len(ps) - 1)
                return last
            return pe.do(go, *after)

        def transposes(jobs, *after):
            def go(e):
                for o, i in jobs:
                    last = e.transpose(o, i, ident[:])
                return last
            return pe.do(go, after, ld("ident"))

        def blk(i):
            return slice(i * P, (i + 1) * P)

        def token_sums(chunks, column, *after):
            sq = []
            for x, t in chunks:
                tile, free = tiles.take()
                sq.append((tile, act.do(lambda e, o=tile, x=x: e.activation(o[:], x, ACT.Square), free, t)))
            bank, free = gen.take()
            t = mms([(bank[:, i:i + 1], [(s[:, blk(i)], column) for s, _ in sq]) for i in range(BLK)],
                    free, [t for _, t in sq], ld("cols"), after)
            for s, _ in sq:
                tiles.give(s, t)
            return bank, t

        def over_tokens(r, t_r):
            bank, free = gen.take()
            t = mms([(bank[:, blk(i)], [(r[:, i:i + 1].broadcast_to([P, P]), ident[:])])
                     for i in range(BLK)], free, t_r, ld("ident"))
            return bank, t

        def rsqrt_of(bank, t_bank, eps):
            s, free = small.take()
            t = dve.do(lambda e: e.tensor_scalar(s[:, 0:BLK], bank[:, 0:BLK], eps, None, ALU.add),
                       free, t_bank)
            gen.give(bank, t)
            t = pool.do(lambda e: e.tensor_tensor(s[:, 8:8 + BLK], s[:, 0:BLK],
                                                  neg_half.broadcast_to([P, BLK]), ALU.pow), t, ld("cols"))
            return s, t

        def t_major(ap):
            return ap.rearrange("p (t b) -> p t b", b=GB)

        def front(g):
            slot = g % 4
            X = xn[slot]
            xt = []
            s = sem(f"ldx_front{g}")
            for kc in range(KC):
                tile, free = tiles.take()
                sp.dma(s, lambda e, o=tile, kc=kc: e.dma_start(o[:], dram["xT"][kc, :, g, :]), free)
                xt.append((tile, (s, 16 * KC)))
            t_silu = []
            for c in range(IC):
                bank, free = gen.take()
                t = mm(bank[:], [(w["w_in"][:, kc, blk(c)], xt[kc][0][:]) for kc in range(KC)],
                       free, [t for _, t in xt], ld("w_in"))
                if c == IC - 1:
                    for tile, _ in xt:
                        tiles.give(tile, t)
                pad, pfree = xr_slots.take()
                body = pad[:, (NCONV - 1) * GB:]
                t = dve.do(lambda e, o=body, i=bank, c=c: e.tensor_tensor(
                    t_major(o), t_major(i[:]),
                    w["temb"][:, c, g * GB:(g + 1) * GB].unsqueeze(1).broadcast_to([P, T, GB]), ALU.add),
                    t, pfree, zeroed, ld("temb"))
                gen.give(bank, t)
                yield
                t = act.do(lambda e, i=body, c=c: e.activation(
                    X[:, c, :], i, ACT.Identity, scale=w["w_conv"][:, c, NCONV - 1:NCONV],
                    bias=w["vecs"][:, 0, c:c + 1]), t, xn_free[slot], ld("w_conv", "vecs"))
                for k in range(NCONV - 1):
                    t = dve.do(lambda e, i=pad, c=c, k=k: e.scalar_tensor_tensor(
                        X[:, c, :], i[:, k * GB:k * GB + TOK], w["w_conv"][:, c, k:k + 1], X[:, c, :],
                        ALU.mult, ALU.add), t)
                xr_slots.give(pad, t)
                t_silu.append(act.do(lambda e, c=c: e.activation(X[:, c, :], X[:, c, :], ACT.Silu), t))
                yield
            bank, free = gen.take()
            t = mm(bank[:], [(w["mean_mat"][:], X[:, c, :]) for c in range(IC)], free, t_silu, ld("mean_mat"))
            t_c = [dve.do(lambda e, c=c, i=bank: e.tensor_tensor(X[:, c, :], X[:, c, :], i[:], ALU.subtract), t)
                   for c in range(IC)]
            gen.give(bank, t_c)
            yield
            bank, t = token_sums([(X[:, c, :], t_c[c]) for c in range(IC)], col_ln)
            r, t = rsqrt_of(bank, t, EPS_LN)
            bank, t = over_tokens(r[:, 8:8 + BLK], t)
            small.give(r, t)
            yield
            t_c = [dve.do(lambda e, c=c, i=bank: e.scalar_tensor_tensor(
                X[:, c, :], X[:, c, :], w["vecs"][:, 1, c:c + 1], i[:], ALU.mult, ALU.mult), t)
                for c in range(IC)]
            gen.give(bank, t_c)
            t_x = [act.do(lambda e, c=c: e.activation(
                X[:, c, :], X[:, c, :], ACT.Identity, bias=w["vecs"][:, 2, c:c + 1]), t_c[c])
                for c in range(IC)]
            yield
            bank, t = token_sums([(X[:, c, :], t_x[c]) for c in range(IC)], col_one)
            nrm, free = small.take()
            t = dve.do(lambda e, o=nrm, i=bank: e.tensor_scalar(o[:, 0:BLK], i[:, 0:BLK], 1.0, None, ALU.min),
                       free, t)
            gen.give(bank, t)
            t_n = pool.do(lambda e, o=nrm: e.tensor_tensor(
                o[:, 8:8 + BLK], o[:, 0:BLK], half.broadcast_to([P, BLK]), ALU.pow), t)
            bank, free = gen.take()
            t = mms([(bank[:, i * NS:(i + 1) * NS], [(X[:, c, blk(i)], w["w_xb"][:, c, :]) for c in range(IC)])
                     for i in range(BLK)], free, t_x, ld("w_xb"))
            bt, free = small.take()
            t = dve.do(lambda e, o=bt, i=bank, n=nrm: e.tensor_tensor(
                o[:].rearrange("p (i n) -> p i n", n=NS), i[:, 0:BLK * NS].rearrange("p (i n) -> p i n", n=NS),
                n[:, 8:8 + BLK].unsqueeze(2).broadcast_to([P, BLK, NS]), ALU.mult), free, t, t_n)
            gen.give(bank, t)
            small.give(nrm, t)
            yield
            bank, free = gen.take()
            t = mms([(bank[:, i * 64:(i + 1) * 64], [(w["sel"][:, i, :], bt[:])]) for i in range(BLK)],
                    free, t, ld("sel"))
            small.give(bt, t)
            tile, free = tiles.take()
            hi = tile[:, 0:256]
            t = dve.do(lambda e, o=hi, i=bank: e.tensor_copy(o.bitcast(F32R), i[:, 0:256]), free, t)
            b4v = b4[slot][:].rearrange("p (k s) n -> p s k n", s=4)

            def rows(ap, a, z):
                return ap[a:z].rearrange("p (s k n) -> p s k n", s=4, n=NS)
            t1 = dve.do(lambda e, i=hi: e.tensor_copy(b4v[0:64], rows(i, 0, 64)), t, coef_free[slot])
            t2 = dve.do(lambda e, i=hi, ps=bank: e.tensor_tensor(
                b4v[64:P], rows(ps[:, 0:256], 64, P), rows(i, 64, P), ALU.subtract), t, coef_free[slot])
            gen.give(bank, t1, t2)
            tiles.give(tile, t1, t2)
            yield
            bank, free = gen.take()
            t = mm(bank[0:48, :], [(w["w_xcd"][:, c, :], X[:, c, :]) for c in range(IC)], free, t_x, ld("w_xcd"))
            tile, free = tiles.take()
            t_cp = act.do(lambda e, i=bank: e.activation(
                cd_pack[0:NS].rearrange("p b t -> p t b"), t_major(i[0:NS, :]), ACT.Copy), t, cd_free[0])
            t_dt = act.do(lambda e, o=tile, i=bank: e.activation(o[32:48, :], i[32:48, :], ACT.Copy), t, free)
            gen.give(bank, t_cp, t_dt)
            bank, free = gen.take()
            t = mm(bank[32:48, :], [(w["dt_w"][32:48, 0:NS], tile[32:48, :])], free, t_dt, ld("dt_w"))
            t = act.do(lambda e, o=tile, i=bank: e.activation(
                o[32:48, :], i[32:48, :], ACT.Tanh, bias=w["dt_w"][32:48, NS:NS + 1]), t)
            gen.give(bank, t)
            t = dve.do(lambda e, i=tile: e.tensor_scalar(
                cd_pack[32:48].rearrange("p b t -> p t b"), t_major(i[32:48, :]), na[32:48, 1:2], 1.0,
                ALU.mult, ALU.add), t, t_na, cd_free[0])
            tiles.give(tile, t)
            s = sem(f"coef{g}")
            for b in range(GB):
                sp.dma(s, lambda e, b=b: e.dma_start(cc[slot][b * NS:(b + 1) * NS, :], cd_pack[0:NS, b, :]),
                       t_cp, coef_free[slot])
                sp.dma(s, lambda e, b=b: e.dma_start(ad[slot][b * NS:(b + 1) * NS, :], cd_pack[32:48, b, :]),
                       t, coef_free[slot])
            t_coef = (s, 16 * 2 * GB)
            cd_free[0] = [t_coef]
            ready[g] = [t_x, t1, t2, t_coef]
            yield

        pre_free, u_free, y_free = ([[], []] for _ in range(3))
        xq_free, ytok_free = [], []
        xrow_free, wu_free, cdiag_free = ([[[], []], [[], []]] for _ in range(3))
        h_free = [[[] for _ in range(RING_H)] for _ in range(2)]
        scanned = [None] * GROUPS

        def scan(pair):
            slots = [(2 * pair + ch) % 4 for ch in range(2)]
            rdy = [ready[2 * pair + ch] for ch in range(2)]
            h_t = [dve.do(lambda e, ch=ch: e.memset(hs[ch][-1][:], 0.0), h_free[ch][-1]) for ch in range(2)]
            in_t = [None, None]
            cd_t = [None, None]
            x_read = [[], []]
            out_t = [[], []]
            b4_read = [[], []]

            def lay_out(ch, k):
                slot, i, q = slots[ch], k % 2, xq
                src = xn[slot][:, :, 32 * k:32 * k + 32].unsqueeze(2).broadcast_to([P, IC, 2, 32])
                t_hi = act.do(lambda e: e.activation(q[:, :, :, 0, :], src, ACT.Copy), rdy[ch], list(xq_free))
                t_lo = pool.do(lambda e: e.tensor_tensor(
                    q[:, :, :, 1, :], src, q[:, :, :, 0, :].bitcast(F32), ALU.subtract), t_hi)
                bank, bfree = x_ps.take()
                t = mms([(bank[:, blk(c)], [(q[:, c].rearrange("p a b r -> p (a b r)"), ident_r[:])])
                         for c in range(IC)], bfree, t_hi, t_lo, t_identr)
                xq_free[:] = [t]
                x_read[ch] = [t_hi, t_lo]
                t_row = act.do(lambda e: e.activation(xrow[ch][i][:], bank[:], ACT.Copy),
                               t, xrow_free[ch][i])
                x_ps.give(bank, t_row)
                t_wu = pool.do(lambda e: e.tensor_tensor(
                    wu[ch][i][:], b4[slot][:, k, :].unsqueeze(1).broadcast_to([P, 32, NS]),
                    w["wu_mask"][:].unsqueeze(2).broadcast_to([P, 32, NS]), ALU.mult),
                    wu_free[ch][i], rdy[ch], ld("wu_mask"))
                b4_read[ch] = [t_wu]
                in_t[ch] = [t_row, t_wu]
                if k % 4 == 0:
                    ring = (k // 4) % 2
                    cd_t[ch] = []
                    for qd in range(4):
                        t0 = 4 * k + 4 * qd
                        cd_t[ch].append(dve.do(lambda e, qd=qd, t0=t0: e.tensor_tensor(
                            cdiag[ch][ring][:, 4 * qd:4 * qd + 4, 8 * qd:8 * qd + 8],
                            cc[slot][:, t0:t0 + 4].unsqueeze(2).broadcast_to([P, 4, GB]),
                            w["c_mask"][:].unsqueeze(1).broadcast_to([P, 4, GB]), ALU.mult),
                            cdiag_free[ch][ring], rdy[ch], t_zero_cd, ld("c_mask")))

            def read_out(ch, k, h_ticks):
                ring, q = (k // 4) % 2, k % 4

                def go(e):
                    for j in range(4):
                        last = e.matmul(y_ps[ch][32 * j:32 * j + 32, :], cdiag[ch][ring][:, 4 * q + j, :],
                                        hs[ch][(4 * k + j) % RING_H][:], start=q == 0, stop=q == 3)
                    return last
                t = pe.do(go, h_ticks, cd_t[ch], y_free[ch])
                for j in range(4):
                    h_free[ch][(4 * k + j) % RING_H] = [t]
                if q < 3:
                    return
                cdiag_free[ch][ring] = [t]
                blk16 = k // 4
                t = act.do(lambda e: e.activation(ytok[:], y_ps[ch][:], ACT.Copy), t, list(ytok_free))
                y_free[ch] = [t]
                bank, bfree = x_ps.take()
                t = transposes([(bank[:, blk(c)], ytok[:, blk(c)]) for c in range(IC)], t, bfree)
                ytok_free[:] = [t]
                X, cols16 = xn[slots[ch]], blk(blk16)
                t_out = []
                for c in range(IC):
                    t_d = act.do(lambda e, c=c: e.activation(
                        X[:, c, cols16], X[:, c, cols16], ACT.Copy, scale=w["vecs"][:, 3, c:c + 1]),
                        x_read[ch], rdy[ch])
                    view = "p (q j b) -> p q j b"
                    t_out.append(dve.do(lambda e, c=c: e.tensor_tensor(
                        X[:, c, cols16].rearrange(view, q=4, b=GB), X[:, c, cols16].rearrange(view, q=4, b=GB),
                        bank[:, blk(c)].rearrange("p (j q b) -> p q j b", q=4, b=GB), ALU.add), t_d, t))
                x_ps.give(bank, t_out)
                out_t[ch] += t_out

            for ch in range(2):
                lay_out(ch, 0)
            for k in range(NX):
                now = list(in_t)
                h_ticks = [[], []]
                for s in range(STEPS_X):
                    step, i = STEPS_X * k + s, k % 2
                    u_t, pre_t = [None, None], [None, None]
                    for ch in range(2):
                        u_t[ch] = pe.do(lambda e, ch=ch: e.matmul(
                            u_ps[ch][:], wu[ch][i][:].rearrange("p m n -> p (m n)")[:, blk(s)],
                            xrow[ch][i][:], start=True, stop=True), now[ch], u_free[ch])
                        pre_t[ch] = dve.do(lambda e, ch=ch: e.scalar_tensor_tensor(
                            pre[ch][:], hs[ch][(step - 1) % RING_H][:], ad[slots[ch]][:, step:step + 1],
                            u_ps[ch][:], ALU.mult, ALU.add), u_t[ch], h_t[ch], pre_free[ch], rdy[ch])
                        u_free[ch] = [pre_t[ch]]
                    for ch in range(2):
                        h_t[ch] = dve.do(lambda e, ch=ch: e.tensor_scalar(
                            hs[ch][step % RING_H][:], pre[ch][:], CLIP, -CLIP, ALU.min, ALU.max),
                            pre_t[ch], h_free[ch][step % RING_H])
                        pre_free[ch] = [h_t[ch]]
                        h_ticks[ch].append(h_t[ch])
                    for ch in range(2):
                        if s == ch and k + 1 < NX:
                            lay_out(ch, k + 1)
                    yield
                for ch in range(2):
                    xrow_free[ch][i] = [u_t[ch]]
                    wu_free[ch][i] = [u_t[ch]]
                    read_out(ch, k, h_ticks[ch])
            for ch in range(2):
                h_free[ch][-1] = [h_free[ch][-1], h_t[ch]]
                coef_free[slots[ch]] = [b4_read[ch], h_t[ch], cd_t[ch]]
                scanned[2 * pair + ch] = out_t[ch]

        def silu_gelu(func, bank, t, dst, free):
            t = act.do(lambda e: e.activation(dst[:], bank[:], func), t, free)
            gen.give(bank, t)
            return t

        def dense(xs, weight, chunks, func):
            res = []
            for m in range(chunks):
                bank, free = gen.take()
                t = mm(bank[:], [(w[weight][:, c, blk(m)], x[:]) for c, (x, _) in enumerate(xs)],
                       free, [t for _, t in xs], ld(weight))
                tile, tfree = tiles.take()
                res.append((tile, silu_gelu(func, bank, t, tile, tfree)))
                last = t
                yield
            for x, _ in xs:
                x_last[id(x)] = last
            return res

        x_last = {}

        def drop(xs):
            for x, _ in xs:
                tiles.give(x, x_last.pop(id(x)))

        def rms_norm(xs, which):
            bank, t = token_sums([(x[:], t) for x, t in xs], col_rms)
            r, t = rsqrt_of(bank, t, EPS_RMS)
            bank, t = over_tokens(r[:, 8:8 + BLK], t)
            small.give(r, t)
            res = []
            for kc, (x, t_x) in enumerate(xs):
                tile, free = tiles.take()
                res.append((tile, dve.do(lambda e, o=tile, x=x, kc=kc: e.scalar_tensor_tensor(
                    o[:], x[:], w["norms"][:, kc, which:which + 1], bank[:], ALU.mult, ALU.mult),
                    free, t, t_x, ld("norms"))))
            gen.give(bank, [t for _, t in res])
            return res

        def attention(h):
            ao = []
            for kc in range(KC):
                ao.append(tiles.take())
            ao_t = [[], []]
            for bp in range(BLK):
                qk, free = gen.take()
                ht = [t for _, t in h]
                t_qk = mm(qk[:], [(h[kc][0][:, blk(bp)], w["w_qk"][:, kc, :]) for kc in range(KC)],
                          free, ht, ld("w_qk"))
                vb, free = gen.take()
                t_v = mms([(vb[64 * par:64 * par + 64, P * b:P * b + P],
                            [(h[kc][0][:, P * bp + T * b:P * bp + T * b + T],
                              w["w_v"][:, kc, :].rearrange("p (h two d) -> p two h d", two=2, d=HD)[:, par])
                             for kc in range(KC)]) for b in range(2) for par in range(2)],
                          free, ld("w_v"))
                vd, vfree = vbd.take()
                t_vd = [act.do(lambda e, par=par: e.activation(
                    vd[64 * par:64 * par + 64, :, :, par, :].rearrange("p b h d -> p (b h) d"),
                    vb[64 * par:64 * par + 64, 0:256].rearrange("p (x d) -> p x d", d=HD), ACT.Copy),
                    t_v, vfree, t_zero_v) for par in range(2)]
                gen.give(vb, t_vd)
                sq, free = tiles.take()
                t = act.do(lambda e: e.activation(sq[:], qk[:], ACT.Square), t_qk, free)
                ss, sfree = small.take()
                t = dve.do(lambda e: e.tensor_reduce(
                    ss[:, 0:32], sq[:].rearrange("p (h d) -> p h d", d=HD), AX, ALU.add), t, sfree)
                tiles.give(sq, t)
                t = dve.do(lambda e: e.tensor_scalar(ss[:, 0:32], ss[:, 0:32], 1.0 / HD, EPS_RMS,
                                                     ALU.mult, ALU.add), t)
                t = pool.do(lambda e: e.tensor_tensor(
                    ss[:, 32:64], ss[:, 0:32], neg_half.broadcast_to([P, 32]), ALU.pow), t, ld("cols"))
                qkn, free = tiles.take()
                t = dve.do(lambda e: e.tensor_tensor(
                    qkn[:].rearrange("p (h d) -> p h d", d=HD), qk[:].rearrange("p (h d) -> p h d", d=HD),
                    ss[:, 32:64].unsqueeze(2).broadcast_to([P, 32, HD]), ALU.mult), t, free)
                gen.give(qk, t)
                small.give(ss, t)
                yield
                bank, free = gen.take()
                t = transposes([(bank[:, blk(i)], qkn[:, blk(i)]) for i in range(4)], t, free)
                tiles.give(qkn, t)
                qkt, free = tiles.take()
                t_qt = [act.do(lambda e, i=i: e.activation(
                    qkt[:, 256 * i:256 * i + 256], bank[:, 256 * i:256 * i + 256], ACT.Copy,
                    scale=w["qkn"][:, i:i + 1]), t, free, ld("qkn")) for i in range(2)]
                gen.give(bank, t_qt)
                scores, t_s = [], []
                for c in range(KC):
                    kd = []
                    for b in range(2):
                        kbd, free = tiles.take()
                        kd.append((kbd, pool.do(lambda e, o=kbd, c=c, b=b: e.tensor_tensor(
                            o[:].rearrange("p (h k) -> p h k", k=T),
                            qkt[:, 256 + P * c + T * b:256 + P * c + T * b + T].unsqueeze(1).broadcast_to([P, 8, T]),
                            w["head_mask"][:].unsqueeze(2).broadcast_to([P, 8, T]), ALU.mult),
                            t_qt, free, ld("head_mask"))))
                    bank, free = gen.take()
                    t = mms([(bank[T * b:T * b + T, :],
                              [(qkt[:, P * c + T * b:P * c + T * b + T], kd[b][0][:])]) for b in range(2)],
                            free, t_qt, [t for _, t in kd])
                    for x, _ in kd:
                        tiles.give(x, t)
                    sc, free = tiles.take()
                    scv = sc[:].rearrange("p (h k) -> p h k", k=T)
                    t_m = dve.do(lambda e, i=bank, o=scv: e.scalar_tensor_tensor(
                        o, i[:].rearrange("p (h k) -> p h k", k=T), HD ** -0.5,
                        w["causal"][:].unsqueeze(1).broadcast_to([P, 8, T]), ALU.mult, ALU.add),
                        t, free, ld("causal"))
                    gen.give(bank, t_m)
                    scores.append((sc, scv, t_m))
                    t_s.append(t)
                    yield
                tiles.give(qkt, t_s)
                st, sfree = small.take()
                probs = []
                for c, (sc, scv, t) in enumerate(scores):
                    m = st[:, 8 * c:8 * c + 8]
                    t = dve.do(lambda e, m=m, i=scv: e.tensor_reduce(m, i, AX, ALU.max), t, sfree)
                    t = pool.do(lambda e, m=m, i=scv: e.tensor_tensor(
                        i, i, m.unsqueeze(2).broadcast_to([P, 8, T]), ALU.subtract), t)
                    t = act.do(lambda e, i=sc: e.activation(i[:], i[:], ACT.Exp), t)
                    t_sum = dve.do(lambda e, c=c, i=scv: e.tensor_reduce(
                        st[:, 16 + 8 * c:24 + 8 * c], i, AX, ALU.add), t)
                    bank, free = gen.take()
                    t = transposes([(bank[:, blk(i)], sc[:, blk(i)]) for i in range(4)], t, free)
                    tiles.give(sc, t, t_sum)
                    pt, free = tiles.take()
                    t_p = act.do(lambda e, o=pt, i=bank: e.activation(o[:], i[:], ACT.Copy), t, free)
                    gen.give(bank, t_p)
                    probs.append((pt, t_p))
                    sums = t_sum
                    yield
                t_r = dve.do(lambda e: e.reciprocal(st[:, 32:48], st[:, 16:32]), sums)
                ob, free = gen.take()
                t = mms([(ob[T * b:T * b + T, 32 * hp:32 * hp + 32],
                          [(probs[hp // 4][0][:, P * (hp % 4) + T * b:P * (hp % 4) + T * b + T],
                            vd[:, b, hp].rearrange("p two d -> p (two d)"))])
                         for hp in range(8) for b in range(2)], free, [t for _, t in probs], t_vd)
                vbd.give(vd, t)
                for x, _ in probs:
                    tiles.give(x, t)
                on, free = tiles.take()
                t = dve.do(lambda e: e.tensor_tensor(
                    on[:, 0:C].rearrange("p (h d) -> p h d", d=HD), ob[:, 0:C].rearrange("p (h d) -> p h d", d=HD),
                    st[:, 32:48].unsqueeze(2).broadcast_to([P, HEADS, HD]), ALU.mult), t, t_r, free)
                gen.give(ob, t)
                small.give(st, t)
                bank, free = gen.take()
                t = transposes([(bank[:, blk(i)], on[:, blk(i)]) for i in range(KC)], t, free)
                tiles.give(on, t)
                for kc in range(KC):
                    ao_t[kc].append(act.do(lambda e, kc=kc, bp=bp: e.activation(
                        ao[kc][0][:, blk(bp)], bank[:, blk(kc)], ACT.Copy), t, ao[kc][1]))
                gen.give(bank, ao_t[0][-1], ao_t[1][-1])
                last_h = [t_qk, t_v]
                yield
            for x, _ in h:
                tiles.give(x, last_h)
            return [(ao[kc][0], ao_t[kc]) for kc in range(KC)]

        def top_two(xf):
            bank, free = gen.take()
            nb = BLK * EXPERTS
            t = mms([(bank[:, i * EXPERTS:(i + 1) * EXPERTS],
                      [(xf[kc][0][:, blk(i)], w["w_gate"][:, kc, :]) for kc in range(KC)])
                     for i in range(BLK)], free, [t for _, t in xf], ld("w_gate"))
            a, afree = small.take()
            d, dfree = small.take()
            f, ffree = small.take()
            pr, st, wt = a[:, 0:nb], a[:, 16:20], a[:, 32:32 + nb]

            def v(ap):
                return ap.rearrange("p (i e) -> p i e", e=EXPERTS)

            def per(ap):
                return ap.unsqueeze(2).broadcast_to([P, BLK, EXPERTS])
            t = dve.do(lambda e: e.tensor_scalar(pr, bank[:, 0:nb], FMAX, -FMAX, ALU.min, ALU.max), t, afree)
            gen.give(bank, t)
            t = dve.do(lambda e: e.tensor_reduce(st, v(pr), AX, ALU.max), t)
            t = dve.do(lambda e: e.tensor_tensor(v(pr), v(pr), per(st), ALU.subtract), t)
            t = act.do(lambda e: e.activation(pr, pr, ACT.Exp), t)
            t = dve.do(lambda e: e.tensor_reduce(st, v(pr), AX, ALU.add), t)
            t = dve.do(lambda e: e.reciprocal(st, st), t)
            t = dve.do(lambda e: e.tensor_tensor(v(pr), v(pr), per(st), ALU.mult), t)
            t_before = []
            for dst, free, op, which in ((d, dfree, ALU.is_ge, 0), (f, ffree, ALU.is_gt, 1)):
                for i in range(BLK):
                    one = pr[:, 4 * i:4 * i + 4]
                    t2 = dve.do(lambda e, dst=dst, i=i, one=one, op=op: e.tensor_tensor(
                        v(dst[:, 16 * i:16 * i + 16]), one.unsqueeze(1).broadcast_to([P, 4, 4]),
                        one.unsqueeze(2).broadcast_to([P, 4, 4]), op), t, free)
                    t_before.append(t2)
                t2 = dve.do(lambda e, dst=dst, which=which: e.tensor_tensor(
                    dst[:].rearrange("p (i m) -> p i m", m=16), dst[:].rearrange("p (i m) -> p i m", m=16),
                    w["rank"][:, which, :].unsqueeze(1).broadcast_to([P, BLK, 16]), ALU.mult),
                    t_before[-BLK:], ld("rank"))
                t_before.append(t2)
            t2 = dve.do(lambda e: e.tensor_tensor(d[:], d[:], f[:], ALU.add), t_before)
            small.give(f, t2)
            t2 = dve.do(lambda e: e.tensor_reduce(wt, d[:].rearrange("p (m j) -> p m j", j=4), AX, ALU.add), t2)
            small.give(d, t2)
            t = dve.do(lambda e: e.scalar_tensor_tensor(wt, wt, TOPK - 0.5, pr, ALU.is_lt, ALU.mult), t2)
            t = dve.do(lambda e: e.tensor_reduce(st, v(wt), AX, ALU.add), t)
            t = dve.do(lambda e: e.tensor_scalar(st, st, EPS_TOP, None, ALU.add), t)
            t = dve.do(lambda e: e.reciprocal(st, st), t)
            t = dve.do(lambda e: e.tensor_tensor(v(wt), v(wt), per(st), ALU.mult), t)
            return a, wt, t

        outs = Slots([sb(f"acc{i}", (P, BLK, C)) for i in range(1)])

        def back(g):
            slot = g % 4
            X = xn[slot]
            xt = []
            s = sem(f"ldx_back{g}")
            for kc in range(KC):
                tile, free = tiles.take()
                sp.dma(s, lambda e, o=tile, kc=kc: e.dma_start(o[:], dram["xT"][kc, :, g, :]), free)
                xt.append((tile, (s, 16 * KC)))
            acc, free_acc = outs.take()
            s_acc = sem(f"ld_acc{g}")
            sp.dma(s_acc, lambda e: e.dma_start(
                acc[:], dram["x"][g * TOK:(g + 1) * TOK, :].rearrange("(i p) c -> p i c", p=P)), free_acc)
            t_z = []
            for c in range(IC):
                bank, free = gen.take()
                t = mm(bank[:], [(w["w_in"][:, kc, DI + P * c:DI + P * c + P], xt[kc][0][:]) for kc in range(KC)],
                       free, [t for _, t in xt], ld("w_in"))
                sg, sfree = tiles.take()
                t_sg = silu_gelu(ACT.Silu, bank, t, sg, sfree)
                t_z.append(pool.do(lambda e, c=c, i=sg: e.tensor_tensor(X[:, c, :], X[:, c, :], i[:], ALU.mult),
                                   t_sg, scanned[g]))
                tiles.give(sg, t_z[-1])
                yield
            for tile, _ in xt:
                tiles.give(tile, t)
            x1 = []
            for m in range(KC):
                bank, free = gen.take()
                t = mm(bank[:], [(w["w_out"][:, c, blk(m)], X[:, c, :]) for c in range(IC)],
                       free, t_z, ld("w_out"))
                tile, tfree = tiles.take()
                t_x = act.do(lambda e, o=tile, i=bank: e.activation(
                    o[:].rearrange("p (b t) -> p t b", t=T), t_major(i[:]), ACT.Copy), t, tfree)
                gen.give(bank, t_x)
                x1.append((tile, t_x))
                yield
            xn_free[slot] = [t]
            h = rms_norm(x1, 0)
            yield
            ao = yield from attention(h)
            for m in range(KC):
                bank, free = gen.take()
                lo = KEPT if m == 0 else 0
                t = mm(bank[lo:, :], [(w["w_o"][:, kc, P * m + lo:P * m + P], ao[kc][0][:]) for kc in range(KC)],
                       free, [t for _, t in ao], ld("w_o"))
                t_x = dve.do(lambda e, o=x1[m][0], i=bank, lo=lo: e.tensor_tensor(
                    o[lo:, :], o[lo:, :], i[lo:, :], ALU.add), t, x1[m][1], [t for _, t in h])
                gen.give(bank, t_x)
                x1[m] = (x1[m][0], [t_x, x1[m][1]])
            for tile, _ in ao:
                tiles.give(tile, t)
            yield
            xf = rms_norm(x1, 1)
            t_acc = [(s_acc, 16)]
            for i2 in range(2):
                bank, free = gen.take()
                t = transposes([(bank[:, P * (2 * j + kc):P * (2 * j + kc) + P], x1[kc][0][:, blk(2 * i2 + j)])
                                for j in range(2) for kc in range(KC)], free, x1[0][1], x1[1][1])
                t_a = dve.do(lambda e, i2=i2, i=bank: e.tensor_tensor(
                    acc[:, 2 * i2:2 * i2 + 2, :], acc[:, 2 * i2:2 * i2 + 2, :],
                    i[:].rearrange("p (i c) -> p i c", c=C), ALU.add), t, t_acc[0])
                gen.give(bank, t_a)
                t_acc.append(t_a)
            for tile, _ in x1:
                tiles.give(tile, t, [t for _, t in xf])
            yield
            route, wt, t_wt = top_two(xf)
            yield
            last_add = [t_acc[1], t_acc[1], t_acc[2], t_acc[2]]

            def expert(index, hidden, weight):
                for i2 in range(2):
                    bank, free = gen.take()
                    t = mms([(bank[:, MOD * j:MOD * j + MOD],
                              [(x[:, blk(2 * i2 + j)], w[weight][:, c, :]) for c, (x, _) in enumerate(hidden)])
                             for j in range(2)], free, [t for _, t in hidden], ld(weight))
                    t_a = []
                    for j in range(2):
                        i = 2 * i2 + j
                        last_add[i] = dve.do(lambda e, i=i, j=j, ps=bank: e.scalar_tensor_tensor(
                            acc[:, i, KEPT:], ps[:, MOD * j:MOD * j + MOD],
                            wt[:, EXPERTS * i + index:EXPERTS * i + index + 1], acc[:, i, KEPT:],
                            ALU.mult, ALU.add), t, t_wt, last_add[i])
                        t_a.append(last_add[i])
                    gen.give(bank, t_a)
                    yield
                for x, _ in hidden:
                    tiles.give(x, t)

            hid = yield from dense(xf, "e1_w1", IC, ACT.Silu)
            gated = []
            for m in range(IC):
                bank, free = gen.take()
                t = mm(bank[:], [(w["e1_w2"][:, kc, blk(m)], xf[kc][0][:]) for kc in range(KC)], free, ld("e1_w2"))
                t = dve.do(lambda e, o=hid[m][0], i=bank: e.tensor_tensor(o[:], o[:], i[:], ALU.mult), t, hid[m][1])
                gen.give(bank, t)
                gated.append((hid[m][0], t))
                yield
            yield from expert(1, gated, "e1_down")
            hid = yield from dense(xf, "e0_up", IC, ACT.Gelu)
            yield from expert(0, hid, "e0_down")
            hid = yield from dense(xf, "e2_l1", IC, ACT.Gelu)
            for weight in ("e2_l2", "e2_l3"):
                nxt = yield from dense(hid, weight, IC, ACT.Gelu)
                drop(hid)
                hid = nxt
            yield from expert(2, hid, "e2_l4")
            low = yield from dense(xf, "e3_down", KC, ACT.Gelu)
            drop(xf)
            hid = yield from dense(low, "e3_up", IC, ACT.Gelu)
            drop(low)
            yield from expert(3, hid, "e3_out")
            small.give(route, last_add)
            s_out = sem("stores")
            sp.dma(s_out, lambda e: e.dma_start(
                out[g * TOK:(g + 1) * TOK, :].rearrange("(i p) c -> p i c", p=P), acc[:]), last_add)
            outs.give(acc, (s_out, 16 * (g + 1)))

        def in_turn(stages):
            for name, steps in stages:
                while advance(name, steps):
                    yield

        for _ in in_turn([("front0", front(0)), ("front1", front(1))]):
            pass
        pairs = GROUPS // 2
        for pair in range(pairs):
            side = []
            if pair > 0:
                side += [(f"back{g}", back(g)) for g in (2 * pair - 2, 2 * pair - 1)]
            if pair + 1 < pairs:
                side += [(f"front{g}", front(g)) for g in (2 * pair + 2, 2 * pair + 3)]
            n_side = SIDE_BACK * 2 * (pair > 0) + SIDE_FRONT * 2 * (pair + 1 < pairs)
            beside, main = in_turn(side), scan(pair)
            due = 0.0
            while advance(f"scan{pair}", main):
                due += n_side / T
                while due >= 1:
                    next(beside, None)
                    due -= 1
            for _ in beside:
                COUNT[0] += 1
        for _ in in_turn([(f"back{g}", back(g)) for g in (GROUPS - 2, GROUPS - 1)]):
            pass

        sp.wait((sem("stores"), 16 * GROUPS))


SIDE_BACK, SIDE_FRONT = 80, 15
COUNT = [0]


def chunked(a, parts):
    return np.ascontiguousarray(a.reshape(parts, P, -1).transpose(1, 0, 2))


def lay_weights(v):
    c, f = (lambda n: v["L0_cond_" + n]), (lambda n: v["L0_ffn_" + n])
    d = {}
    d["w_in"] = chunked(c("W_in").T, KC)
    wx = c("W_xproj").T
    d["w_xb"] = chunked(wx[:, 0:NS], IC)
    gap = np.zeros((DI, NS), wx.dtype)
    d["w_xcd"] = chunked(np.concatenate([wx[:, NS:2 * NS], gap, wx[:, 2 * NS:]], 1), IC)
    d["w_out"] = chunked(c("W_out").T, IC)
    d["w_qk"] = chunked(np.concatenate([f("wq").T, f("wk").T], 1), KC)
    for name, key, n in (("w_v", "wv", KC), ("w_o", "wo", KC), ("w_gate", "gate_w", KC), ("e0_up", "e0_up", KC),
                         ("e1_w1", "e1_w1", KC), ("e1_w2", "e1_w2", KC), ("e2_l1", "e2_l1", KC),
                         ("e2_l2", "e2_l2", IC), ("e2_l3", "e2_l3", IC), ("e3_down", "e3_down", KC),
                         ("e3_up", "e3_up", KC)):
        d[name] = chunked(f(key).T, n)
    for name in ("e0_down", "e1_down", "e2_l4", "e3_out"):
        d[name] = chunked(f(name).T[:, KEPT:], IC)
    d["temb"] = chunked(v["cond_2048"].T, IC)
    d["w_conv"] = chunked(c("W_conv").reshape(DI, NCONV), IC)
    d["vecs"] = np.ascontiguousarray(np.stack(
        [c(n).reshape(IC, P).T for n in ("b_conv", "ln_g", "ln_b", "D")], 1))
    d["norms"] = np.ascontiguousarray(np.stack([f(n).reshape(KC, P).T for n in ("n1_w", "n2_w")], 2))
    d["qkn"] = np.ascontiguousarray(np.stack([np.tile(f(n), P // HD) for n in ("qn_w", "kn_w")], 1))
    dt_w = np.zeros((P, NS + 2), wx.dtype)
    dt_w[32:48, 0:NS] = c("W_dt").T
    dt_w[32:48, NS] = c("b_dt")
    dt_w[32:48, NS + 1] = c("A_log")
    d["dt_w"] = dt_w
    return d


def lay_constants():
    d, i = {}, np.arange(P)
    d["ident"] = np.eye(P)
    d["sel"] = (i[:, None, None] == 32 * np.arange(BLK)[None, :, None] + (i % 32)[None, None, :])
    d["mean_mat"] = np.full((P, P), 1.0 / DI)
    d["cols"] = np.tile([1.0 / DI, 1.0 / C, 1.0, -0.5, 0.5], (P, 1))
    d["wu_mask"] = (i % 32)[:, None] == np.arange(32)[None, :]
    d["c_mask"] = (i // NS)[:, None] == np.arange(GB)[None, :]
    d["causal"] = np.where(np.arange(T)[None, :] <= (i % T)[:, None], 0.0, MASKED)
    d["head_mask"] = (i // HD)[:, None] == np.arange(8)[None, :]
    e = np.arange(EXPERTS)
    lower = (e[None, :] < e[:, None]).reshape(-1)
    upper = (e[None, :] > e[:, None]).reshape(-1)
    d["rank"] = np.tile(np.stack([lower, upper])[None], (P, 1, 1))
    return {k: np.ascontiguousarray(a.astype(np.float32)) for k, a in d.items()}


def kernel(**inputs):
    import concourse.bacc as bacc
    from concourse.bass_utils import run_bass_kernel_spmd

    v = {k: np.asarray(a) for k, a in inputs.items()}
    arrays = {**lay_weights(v), **lay_constants()}
    x = v["x"]
    arrays["xT"] = np.ascontiguousarray(
        x.reshape(GROUPS, GB, T, KC, P).transpose(3, 4, 0, 2, 1).reshape(KC, P, GROUPS, TOK))
    arrays["x"] = np.ascontiguousarray(x.reshape(B * T, C))
    for k, s in W_SHAPES.items():
        assert arrays[k].shape == (P,) + s, (k, arrays[k].shape)

    nc = bacc.Bacc("TRN2", target_bir_lowering=False, num_devices=1)
    dram = {k: nc.dram_tensor(f"in_{k}", a.shape, mybir.dt.from_np(a.dtype), kind="ExternalInput").ap()
            for k, a in arrays.items()}
    out = nc.dram_tensor("out_y", (B * T, C), F32, kind="ExternalOutput").ap()
    build_program(nc, dram, out)
    r = run_bass_kernel_spmd(nc, [{f"in_{k}": a for k, a in arrays.items()}], core_ids=[0])
    return r.results[0]["out_y"].reshape(B, T, C)
```

```python
from collections import namedtuple
from contextlib import ExitStack

import numpy as np

import concourse.bass as bass
from concourse import mybir

F32 = mybir.dt.float32
F32R = mybir.dt.float32r
ACT = mybir.ActivationFunctionType
ALU = mybir.AluOpType
AX = mybir.AxisListType.X

P = 128
B, T, C = 64, 64, 256
DI = 512
NS = 16
GROUPS = 8
GB = B // GROUPS
TOK = GB * T
KC, IC = C // P, DI // P
BLK = TOK // P
HEADS, HD = 16, 16
EXPERTS, TOPK = 4, 2
KEPT = 64
MOD = C - KEPT
STEPS_X = 4
NX = T // STEPS_X
U_BANKS = 2
WRING = 5
PIECE = 2
RING_H = 6
LATENCY, DMA_LATENCY = 0.1, 2.5
XN = 3
CLIP = 10.0
EPS_LN, EPS_RMS, EPS_TOP = 1e-5, 1.1920929e-07, 1e-8
MASKED = -1.0e30
FMAX = 3.4028234663852886e38
NCONV = 4

W_SHAPES = {
    "w_in": (KC, 2 * DI), "w_xb": (IC, NS), "w_xcd": (IC, 48), "w_out": (IC, C),
    "w_qk": (KC, 2 * C), "w_v": (KC, C), "w_o": (KC, C), "w_gate": (KC, EXPERTS),
    "temb": (IC, B), "w_conv": (IC, NCONV), "vecs": (4, IC), "norms": (KC, 2), "qkn": (2,),
    "dt_w": (NS + 2,),
    "ident": (P,), "sel": (BLK, P), "mean_mat": (P,), "cols": (5,), "wu_mask": (32,),
    "c_mask": (GB,), "causal": (T,), "head_mask": (8,), "rank": (2, EXPERTS * EXPERTS),
}
EXPERT_SHAPES = {
    "e1_w1": (KC, DI), "e1_w2": (KC, DI), "e1_down": (IC, MOD), "e0_up": (KC, DI), "e0_down": (IC, MOD),
    "e2_l1": (KC, DI), "e2_l2": (IC, DI), "e2_l3": (IC, DI), "e2_l4": (IC, MOD),
    "e3_down": (KC, C), "e3_up": (KC, DI), "e3_out": (IC, MOD),
}
WSLOT = KC * DI
LOADS = [("w_in", "temb"), ("w_conv", "vecs", "mean_mat", "cols", "ident"),
         ("w_xb", "w_xcd", "dt_w", "sel", "wu_mask", "c_mask"),
         ("w_out", "norms", "w_qk", "w_v", "qkn", "head_mask", "causal", "w_o", "w_gate", "rank")]


Tick = namedtuple("Tick", "sem count at")
WAIT = "blocked"


class Lane:

    def __init__(self, name, engine, new_sem):
        self.name, self.engine, self.new_sem, self.counts, self.seen = name, engine, new_sem, {}, {}
        self.clock = 0.0
        self.phase("setup")

    def phase(self, stage):
        self.key = f"{self.name}_{stage}"

    def wait(self, *after):
        for tick in flat(after):
            if self.seen.get(id(tick.sem), 0) < tick.count:
                self.engine.wait_ge(tick.sem, tick.count)
                self.seen[id(tick.sem)] = tick.count
            self.clock = max(self.clock, tick.at)

    def do(self, build, *after, cost=0.6):
        self.wait(after)
        n = self.counts[self.key] = self.counts.get(self.key, 0) + 1
        sem = self.new_sem(self.key)
        build(self.engine).then_inc(sem, 1)
        self.clock += cost
        return Tick(sem, n, self.clock + LATENCY)

    def go(self, build, *after, cost=0.6):
        yield self, max([t.at for t in flat(after)], default=0.0)
        return self.do(build, *after, cost=cost)

    def dma(self, sem, total, build, *after):
        self.wait(after)
        build(self.engine).then_inc(sem, 16)
        return Tick(sem, total, self.clock + DMA_LATENCY)


def flat(ticks):
    if ticks is None:
        return []
    if isinstance(ticks, Tick):
        return [ticks]
    return [t for part in ticks for t in flat(part)]


class Slots:

    def __init__(self, bufs):
        self.bufs = [(b, []) for b in bufs]

    def take(self):
        while not self.bufs:
            yield WAIT
        first = min(range(len(self.bufs)), key=lambda i: max([t.at for t in self.bufs[i][1]], default=0))
        return self.bufs.pop(first)

    def give(self, buf, *last_readers):
        self.bufs.append((buf, flat(last_readers)))


def build_program(nc, dram, out):
    ctx = ExitStack()
    with ctx:
        def sb(name, shape, dt=F32):
            return ctx.enter_context(nc.sbuf_tensor(name, list(shape), dt))

        sems = {}

        def sem(name):
            if name not in sems:
                sems[name] = ctx.enter_context(nc.semaphore(name))
            return sems[name]

        pe, act, dve, pool, sp = (Lane(n, e, sem) for n, e in (
            ("pe", nc.tensor), ("act", nc.scalar), ("dve", nc.vector), ("pool", nc.gpsimd), ("sp", nc.sync)))
        lanes = (pe, act, dve, pool)


        w = {k: sb(k, (P,) + s) for k, s in W_SHAPES.items()}
        loaded = {}
        for n, batch in enumerate(LOADS):
            s = sem(f"weights{n}")
            for k in batch:
                loaded[k] = sp.dma(s, 16 * len(batch), lambda e: e.dma_start(w[k][:], dram[k]))

        def ld(*names):
            return [loaded[n] for n in names]

        ident, cols = w["ident"], w["cols"]
        col_ln, col_rms, col_one = cols[:, 0:1], cols[:, 1:2], cols[:, 2:3]
        neg_half, half = cols[:, 3:4], cols[:, 4:5]
        ident_r = sb("ident_r", (P, P), F32R)
        na = sb("na", (P, 2))

        scan_inputs = Slots([(sb(f"xn{i}", (P, IC, TOK)), sb(f"ad{i}", (P, T)), sb(f"cc{i}", (P, T)),
                              sb(f"b4{i}", (P, NX, NS))) for i in range(XN)])
        handed = {}
        xr_pad = [sb(f"xr_pad{i}", (P, (T + NCONV - 1) * GB)) for i in range(2)]
        xr_slots = Slots(xr_pad)
        front_tiles = Slots([sb(f"front{i}", (P, 512)) for i in range(5)])
        mid_tiles = [Slots([sb(f"mid{j}_{i}", (P, 512)) for i in range(13)]) for j in range(2)]
        wring = Slots([sb(f"wring{i}", (P, WSLOT)) for i in range(WRING)])
        hidden_tiles = Slots([sb(f"hidden{i}", (P, 512)) for i in range(8)])
        small = Slots([sb(f"small{i}", (P, 64)) for i in range(10)])
        accs = Slots([sb(f"acc{i}", (P, BLK, C)) for i in range(2)])
        vbds = [sb(f"vbd{i}", (P, 2, 8, 2, HD)) for i in range(2)]
        vbd = Slots(vbds)
        cd_packs = Slots([sb("cd_pack", (48, GB, T))])

        xqs = Slots([sb("xq", (P, IC, 2, 2, 32), F32R)])
        xrows = Slots([sb(f"xrow{i}", (P, DI), F32R) for i in range(2)])
        wus = Slots([sb(f"wu{i}", (P, 32, NS), F32R) for i in range(2)])
        hs = [sb(f"h{i}", (P, DI)) for i in range(RING_H)]
        pre = [sb(f"pre{i}", (P, DI)) for i in range(2)]
        ytok = sb("ytok", (P, DI))
        cdiags = [sb(f"cdiag{i}", (P, 16, 32)) for i in range(2)]

        banks = [ctx.enter_context(nc.psum_tensor(f"bank{i}", [P, 512], F32)) for i in range(8)]
        u_ps, y_ps, gen = banks[0:U_BANKS], banks[U_BANKS], Slots(banks[U_BANKS + 1:])

        t_identr = dve.do(lambda e: e.tensor_copy(ident_r[:], ident[:]), ld("ident"))
        zeroed = [dve.do(lambda e, x=x: e.memset(x[:, 0:(NCONV - 1) * GB], 0.0)) for x in xr_pad]
        t_zero_cd = [dve.do(lambda e, x=x: e.memset(x[:], 0.0)) for x in cdiags]
        t_zero_v = [pool.do(lambda e, x=x: e.memset(x[:], 0.0)) for x in vbds]
        t_na = act.do(lambda e: e.activation(na[32:48, 0:1], w["dt_w"][32:48, NS + 1:NS + 2], ACT.Tanh),
                      ld("dt_w"))
        t_na = dve.do(lambda e: e.tensor_scalar(na[32:48, 1:2], na[32:48, 0:1], -0.01, None, ALU.mult),
                      t_na)

        def mm(out_ap, pairs, *after):
            return (yield from mms([(out_ap, pairs)], *after))

        def long_mm(out_ap, pairs, *after):
            pairs = list(pairs)
            for i0 in range(0, len(pairs), PIECE):
                part = pairs[i0:i0 + PIECE]

                def go(e):
                    for i, (lhs, rhs) in enumerate(part, i0):
                        last = e.matmul(out_ap, lhs, rhs, start=i == 0, stop=i == len(pairs) - 1)
                    return last
                t = (yield from pe.go(go, *after, cost=sum(matmul_cost(rhs) for _, rhs in part)))
                if i0 + PIECE < len(pairs):
                    yield
            return t

        def matmul_cost(rhs):
            n = 1
            for x in rhs.shape[1:]:
                n *= x
            return max(n, 128) * (1 if rhs.dtype == F32R else 4) / 2400 if n > 64 or rhs.dtype == F32R else 0.214

        def mms(jobs, *after):
            jobs = [(o, list(ps)) for o, ps in jobs]

            def go(e):
                for o, ps in jobs:
                    for i, (lhs, rhs) in enumerate(ps):
                        last = e.matmul(o, lhs, rhs, start=i == 0, stop=i == len(ps) - 1)
                return last
            return (yield from pe.go(go, *after, cost=sum(matmul_cost(rhs) for _, ps in jobs for _, rhs in ps)))

        def transposes(jobs, *after):
            def go(e):
                for o, i in jobs:
                    last = e.transpose(o, i, ident[:])
                return last
            return (yield from pe.go(go, after, ld("ident"), cost=0.11 * len(jobs)))

        def blk(i):
            return slice(i * P, (i + 1) * P)

        def token_sums(tiles, chunks, column, *after):
            sq = []
            for x, t in chunks:
                tile, free = (yield from tiles.take())
                sq.append((tile, (yield from act.go(lambda e, o=tile, x=x: e.activation(o[:], x, ACT.Square), free, t))))
            bank, free = (yield from gen.take())
            t = (yield from mms([(bank[:, i:i + 1], [(s[:, blk(i)], column) for s, _ in sq]) for i in range(BLK)],
                    free, [t for _, t in sq], ld("cols"), after))
            for s, _ in sq:
                tiles.give(s, t)
            return bank, t

        def over_tokens(r, t_r):
            bank, free = (yield from gen.take())
            t = (yield from mms([(bank[:, blk(i)], [(r[:, i:i + 1].broadcast_to([P, P]), ident[:])])
                     for i in range(BLK)], free, t_r, ld("ident")))
            return bank, t

        def rsqrt_of(bank, t_bank, eps):
            s, free = (yield from small.take())
            t = (yield from dve.go(lambda e: e.tensor_scalar(s[:, 0:BLK], bank[:, 0:BLK], eps, None, ALU.add),
                       free, t_bank))
            gen.give(bank, t)
            t = (yield from pool.go(lambda e: e.tensor_tensor(s[:, 8:8 + BLK], s[:, 0:BLK],
                                                  neg_half.broadcast_to([P, BLK]), ALU.pow), t, ld("cols"), cost=0.4))
            return s, t

        def t_major(ap):
            return ap.rearrange("p (t b) -> p t b", b=GB)

        def front(g):
            (X, decay, c_rows, b4), x_free = yield from scan_inputs.take()
            xt = []
            s = sem(f"ldx_front{g}")
            for kc in range(KC):
                tile, free = (yield from front_tiles.take())
                xt.append((tile, sp.dma(s, 16 * KC, lambda e: e.dma_start(tile[:], dram["xT"][kc, :, g, :]), free)))
            t_silu = []
            for c in range(IC):
                bank, free = (yield from gen.take())
                t = (yield from mm(bank[:], [(w["w_in"][:, kc, blk(c)], xt[kc][0][:]) for kc in range(KC)],
                       free, [t for _, t in xt], ld("w_in")))
                if c == IC - 1:
                    for tile, _ in xt:
                        front_tiles.give(tile, t)
                pad, pfree = (yield from xr_slots.take())
                body = pad[:, (NCONV - 1) * GB:]
                t = (yield from dve.go(lambda e, o=body, i=bank, c=c: e.tensor_tensor(
                    t_major(o), t_major(i[:]),
                    w["temb"][:, c, g * GB:(g + 1) * GB].unsqueeze(1).broadcast_to([P, T, GB]), ALU.add),
                    t, pfree, zeroed, ld("temb")))
                gen.give(bank, t)
                yield
                t = (yield from act.go(lambda e, i=body, c=c: e.activation(
                    X[:, c, :], i, ACT.Identity, scale=w["w_conv"][:, c, NCONV - 1:NCONV],
                    bias=w["vecs"][:, 0, c:c + 1]), t, x_free, ld("w_conv", "vecs")))
                for k in range(NCONV - 1):
                    t = (yield from dve.go(lambda e, i=pad, c=c, k=k: e.scalar_tensor_tensor(
                        X[:, c, :], i[:, k * GB:k * GB + TOK], w["w_conv"][:, c, k:k + 1], X[:, c, :],
                        ALU.mult, ALU.add), t))
                xr_slots.give(pad, t)
                t_silu.append((yield from act.go(lambda e, c=c: e.activation(X[:, c, :], X[:, c, :], ACT.Silu), t)))
                yield
            bank, free = (yield from gen.take())
            t = (yield from mm(bank[:], [(w["mean_mat"][:], X[:, c, :]) for c in range(IC)], free, t_silu, ld("mean_mat")))
            t_c = []
            for c in range(IC):
                t_c.append((yield from dve.go(lambda e: e.tensor_tensor(X[:, c, :], X[:, c, :], bank[:], ALU.subtract), t)))
            gen.give(bank, t_c)
            yield
            bank, t = (yield from token_sums(front_tiles, [(X[:, c, :], t_c[c]) for c in range(IC)], col_ln))
            r, t = yield from rsqrt_of(bank, t, EPS_LN)
            bank, t = yield from over_tokens(r[:, 8:8 + BLK], t)
            small.give(r, t)
            yield
            t_c, t_x = [], []
            for c in range(IC):
                t_c.append((yield from dve.go(lambda e: e.scalar_tensor_tensor(
                    X[:, c, :], X[:, c, :], w["vecs"][:, 1, c:c + 1], bank[:], ALU.mult, ALU.mult), t)))
                t_x.append((yield from act.go(lambda e: e.activation(
                    X[:, c, :], X[:, c, :], ACT.Identity, bias=w["vecs"][:, 2, c:c + 1]), t_c[c])))
            gen.give(bank, t_c)
            yield
            bank, t = (yield from token_sums(front_tiles, [(X[:, c, :], t_x[c]) for c in range(IC)], col_one))
            nrm, free = (yield from small.take())
            t = (yield from dve.go(lambda e, o=nrm, i=bank: e.tensor_scalar(o[:, 0:BLK], i[:, 0:BLK], 1.0, None, ALU.min),
                       free, t))
            gen.give(bank, t)
            t_n = (yield from pool.go(lambda e, o=nrm: e.tensor_tensor(
                o[:, 8:8 + BLK], o[:, 0:BLK], half.broadcast_to([P, BLK]), ALU.pow), t, cost=0.4))
            bank, free = (yield from gen.take())
            t = (yield from mms([(bank[:, i * NS:(i + 1) * NS], [(X[:, c, blk(i)], w["w_xb"][:, c, :]) for c in range(IC)])
                     for i in range(BLK)], free, t_x, ld("w_xb")))
            bt, free = (yield from small.take())
            t = (yield from dve.go(lambda e, o=bt, i=bank, n=nrm: e.tensor_tensor(
                o[:].rearrange("p (i n) -> p i n", n=NS), i[:, 0:BLK * NS].rearrange("p (i n) -> p i n", n=NS),
                n[:, 8:8 + BLK].unsqueeze(2).broadcast_to([P, BLK, NS]), ALU.mult), free, t, t_n))
            gen.give(bank, t)
            small.give(nrm, t)
            yield
            bank, free = (yield from gen.take())
            t = (yield from mms([(bank[:, i * 64:(i + 1) * 64], [(w["sel"][:, i, :], bt[:])]) for i in range(BLK)],
                    free, t, ld("sel")))
            small.give(bt, t)
            tile, free = (yield from front_tiles.take())
            hi = tile[:, 0:256]
            t = (yield from dve.go(lambda e, o=hi, i=bank: e.tensor_copy(o.bitcast(F32R), i[:, 0:256]), free, t))
            b4v = b4[:].rearrange("p (k s) n -> p s k n", s=4)

            def rows(ap, a, z):
                return ap[a:z].rearrange("p (s k n) -> p s k n", s=4, n=NS)
            t1 = (yield from dve.go(lambda e, i=hi: e.tensor_copy(b4v[0:64], rows(i, 0, 64)), t, x_free))
            t2 = (yield from dve.go(lambda e, i=hi, ps=bank: e.tensor_tensor(
                b4v[64:P], rows(ps[:, 0:256], 64, P), rows(i, 64, P), ALU.subtract), t, x_free))
            gen.give(bank, t1, t2)
            front_tiles.give(tile, t1, t2)
            yield
            bank, free = (yield from gen.take())
            t = (yield from mm(bank[0:48, :], [(w["w_xcd"][:, c, :], X[:, c, :]) for c in range(IC)], free, t_x, ld("w_xcd")))
            tile, free = (yield from front_tiles.take())
            cd_pack, cd_free = yield from cd_packs.take()
            t_cp = (yield from act.go(lambda e, i=bank: e.activation(
                cd_pack[0:NS].rearrange("p b t -> p t b"), t_major(i[0:NS, :]), ACT.Copy), t, cd_free))
            t_dt = (yield from act.go(lambda e, o=tile, i=bank: e.activation(o[32:48, :], i[32:48, :], ACT.Copy), t, free))
            gen.give(bank, t_cp, t_dt)
            bank, free = (yield from gen.take())
            t = (yield from mm(bank[32:48, :], [(w["dt_w"][32:48, 0:NS], tile[32:48, :])], free, t_dt, ld("dt_w")))
            t = (yield from act.go(lambda e, o=tile, i=bank: e.activation(
                o[32:48, :], i[32:48, :], ACT.Tanh, bias=w["dt_w"][32:48, NS:NS + 1]), t))
            gen.give(bank, t)
            t = (yield from dve.go(lambda e, i=tile: e.tensor_scalar(
                cd_pack[32:48].rearrange("p b t -> p t b"), t_major(i[32:48, :]), na[32:48, 1:2], 1.0,
                ALU.mult, ALU.add), t, t_na, cd_free))
            front_tiles.give(tile, t)
            s = sem(f"coef{g}")
            for b in range(GB):
                t_coef = sp.dma(s, 32 * GB, lambda e: e.dma_start(
                    c_rows[b * NS:(b + 1) * NS, :], cd_pack[0:NS, b, :]), t_cp, x_free)
                t_coef = sp.dma(s, 32 * GB, lambda e: e.dma_start(
                    decay[b * NS:(b + 1) * NS, :], cd_pack[32:48, b, :]), t, x_free)
            cd_packs.give(cd_pack, t_coef)
            handed["front", g] = ((X, decay, c_rows, b4), [t_x, t1, t2, t_coef])
            yield

        ring_free = {}

        def scan(g):
            while ("front", g) not in handed:
                yield WAIT
            inputs, t_in = handed.pop(("front", g))
            X, decay, c_rows, b4 = inputs
            t_h = (yield from dve.go(lambda e: e.memset(hs[-1][:], 0.0), ring_free.get(("h", RING_H - 1)),
                         ring_free.get(("state", 0)), cost=0.3))
            t_read, t_wu, t_out, t_diag = [], None, [], [None, None]

            def lay_out(k):
                nonlocal t_read, t_wu
                q, qfree = yield from xqs.take()
                src = X[:, :, 32 * k:32 * k + 32].unsqueeze(2).broadcast_to([P, IC, 2, 32])
                t_hi = (yield from act.go(lambda e: e.activation(q[:, :, :, 0, :], src, ACT.Copy), t_in, qfree, cost=0.4))
                t_lo = (yield from pool.go(lambda e: e.tensor_tensor(
                    q[:, :, :, 1, :], src, q[:, :, :, 0, :].bitcast(F32), ALU.subtract), t_hi, cost=0.7))
                wu, wfree = yield from wus.take()
                t_wu = (yield from pool.go(lambda e: e.tensor_tensor(
                    wu[:], b4[:, k, :].unsqueeze(1).broadcast_to([P, 32, NS]),
                    w["wu_mask"][:].unsqueeze(2).broadcast_to([P, 32, NS]), ALU.mult),
                    wfree, t_in, ld("wu_mask"), cost=1.2))
                bank, bfree = yield from gen.take()
                t = (yield from mms([(bank[:, blk(c)], [(q[:, c].rearrange("p a b r -> p (a b r)"), ident_r[:])])
                         for c in range(IC)], bfree, t_hi, t_lo, t_identr))
                xqs.give(q, t)
                t_read = [t_hi, t_lo]
                row, rfree = yield from xrows.take()
                t_row = (yield from act.go(lambda e: e.activation(row[:], bank[:], ACT.Copy), t, rfree))
                gen.give(bank, t_row)
                if k % 4 == 0:
                    ring = (k // 4) % 2
                    for qd in range(4):
                        t0 = 4 * k + 4 * qd
                        t_diag[ring] = (yield from dve.go(lambda e: e.tensor_tensor(
                            cdiags[ring][:, 4 * qd:4 * qd + 4, 8 * qd:8 * qd + 8],
                            c_rows[:, t0:t0 + 4].unsqueeze(2).broadcast_to([P, 4, GB]),
                            w["c_mask"][:].unsqueeze(1).broadcast_to([P, 4, GB]), ALU.mult),
                            ring_free.get(("cdiag", ring)), t_in, t_zero_cd, ld("c_mask"), cost=0.1))
                return row, t_row, wu, t_wu

            def bring_in(step, laid):
                row, t_row, wu, t_wu = laid
                i = step % U_BANKS
                return (yield from mm(u_ps[i][:], [(wu[:].rearrange("p m n -> p (m n)")[:, blk(step % STEPS_X)], row[:])],
                          t_row, t_wu, ring_free.get(("u", i))))

            def read_out(k, t_hs):
                ring, q = (k // 4) % 2, k % 4

                def go(e):
                    for j in range(4):
                        last = e.matmul(y_ps[32 * j:32 * j + 32, :], cdiags[ring][:, 4 * q + j, :],
                                        hs[(4 * k + j) % RING_H][:], start=q == 0, stop=q == 3)
                    return last
                t = (yield from pe.go(go, t_hs, t_diag[ring], ring_free.get(("y", 0)), cost=0.95))
                for j in range(4):
                    ring_free["h", (4 * k + j) % RING_H] = t
                if q < 3:
                    return
                ring_free["cdiag", ring] = t
                t = (yield from act.go(lambda e: e.activation(ytok[:], y_ps[:], ACT.Copy), t, ring_free.get(("ytok", 0))))
                ring_free["y", 0] = t
                bank, bfree = yield from gen.take()
                t = (yield from transposes([(bank[:, blk(c)], ytok[:, blk(c)]) for c in range(IC)], t, bfree))
                ring_free["ytok", 0] = t
                cols16, view = blk(k // 4), "p (q j b) -> p q j b"
                for c in range(IC):
                    t_d = (yield from act.go(lambda e: e.activation(
                        X[:, c, cols16], X[:, c, cols16], ACT.Copy, scale=w["vecs"][:, 3, c:c + 1]),
                        t_read, t_in, cost=0.4))
                    t_out.append((yield from dve.go(lambda e: e.tensor_tensor(
                        X[:, c, cols16].rearrange(view, q=4, b=GB), X[:, c, cols16].rearrange(view, q=4, b=GB),
                        bank[:, blk(c)].rearrange("p (j q b) -> p q j b", q=4, b=GB), ALU.add), t_d, t,
                        cost=0.26)))
                gen.give(bank, t_out[-IC:])

            laid = yield from lay_out(0)
            t_u = [(yield from bring_in(0, laid))]
            late = None
            for k in range(NX):
                nxt, t_hs = None, []
                for s in range(STEPS_X):
                    step = STEPS_X * k + s
                    if s == 0 and k + 1 < NX:
                        nxt = yield from lay_out(k + 1)
                    if s + 1 < STEPS_X:
                        t_u.append((yield from bring_in(step + 1, laid)))
                    elif nxt:
                        t_u.append((yield from bring_in(step + 1, nxt)))
                    if s == 1 and late is not None:
                        yield from read_out(k - 1, late)
                    p, i = pre[step % 2], step % U_BANKS
                    t_p = (yield from dve.go(lambda e: e.scalar_tensor_tensor(
                        p[:], hs[(step - 1) % RING_H][:], decay[:, step:step + 1], u_ps[i][:],
                        ALU.mult, ALU.add), t_u[-2] if step + 1 < T else t_u[-1], t_h,
                        ring_free.get(("pre", step % 2)), t_in, cost=0.66))
                    ring_free["u", i] = t_p
                    t_h = (yield from dve.go(lambda e: e.tensor_scalar(
                        hs[step % RING_H][:], p[:], CLIP, -CLIP, ALU.min, ALU.max),
                        t_p, ring_free.get(("h", step % RING_H)), cost=0.4))
                    ring_free["pre", step % 2] = t_h
                    t_hs.append(t_h)
                xrows.give(laid[0], t_u[-1] if not nxt else t_u[-2])
                wus.give(laid[2], t_u[-1] if not nxt else t_u[-2])
                laid, late = nxt, t_hs
            yield from read_out(NX - 1, late)
            ring_free["state", 0] = t_h
            handed["scan", g] = (inputs, t_out, [t_wu, t_h, t_diag])
            yield

        arrived = []

        def expert_weights(g):
            for name, (parts, n) in EXPERT_SHAPES.items():
                per = min(parts, WSLOT // n)
                for p0 in range(0, parts, per):
                    buf, free = yield from wring.take()
                    nbuf = wring_index[id(buf)]
                    landed[nbuf] += 16
                    view = buf[:, 0:per * n].rearrange("p (c n) -> p c n", n=n)
                    t = sp.dma(sem(f"wring{nbuf}"), landed[nbuf],
                               lambda e: e.dma_start(view, dram[name][:, p0:p0 + per, :]), free)
                    arrived.append((name, buf, view, t))
                    yield sp, sp.clock

        landed = [0] * WRING
        wring_index = {id(b): i for i, (b, _) in enumerate(wring.bufs)}

        def weight_of(name):
            parts, n = EXPERT_SHAPES[name]
            chunks, ticks, bufs = [], [], []
            while len(chunks) < parts:
                while not arrived:
                    yield WAIT
                got, buf, view, t = arrived.pop(0)
                assert got == name
                chunks += [view[:, i, :] for i in range(view.shape[1])]
                ticks.append(t)
                bufs.append(buf)
            return chunks, ticks, bufs

        def drop_weight(bufs, t):
            for b in bufs:
                wring.give(b, t)

        def dense(pool_, xs, weight, chunks, func):
            res = []
            wc, t_w, bufs = yield from weight_of(weight)
            for m in range(chunks):
                bank, free = yield from gen.take()
                t = yield from long_mm(bank[:], [(wc[c][:, blk(m)], x[:]) for c, (x, _) in enumerate(xs)],
                                       free, [t for _, t in xs], t_w)
                tile, tfree = yield from pool_.take()
                t_f = (yield from act.go(lambda e: e.activation(tile[:], bank[:], func), t, tfree))
                gen.give(bank, t_f)
                res.append((tile, t_f))
                yield
            drop_weight(bufs, t)
            return res, t

        def drop(pool_, xs, t):
            for x, _ in xs:
                pool_.give(x, t)

        def rms_norm(tiles, xs, which):
            bank, t = yield from token_sums(tiles, [(x[:], t) for x, t in xs], col_rms)
            r, t = yield from rsqrt_of(bank, t, EPS_RMS)
            yield
            bank, t = yield from over_tokens(r[:, 8:8 + BLK], t)
            small.give(r, t)
            yield
            res = []
            for kc, (x, t_x) in enumerate(xs):
                tile, free = (yield from tiles.take())
                res.append((tile, (yield from dve.go(lambda e, o=tile, x=x, kc=kc: e.scalar_tensor_tensor(
                    o[:], x[:], w["norms"][:, kc, which:which + 1], bank[:], ALU.mult, ALU.mult),
                    free, t, t_x, ld("norms")))))
            gen.give(bank, [t for _, t in res])
            return res

        def attention(tiles, h):
            ao = []
            for kc in range(KC):
                ao.append((yield from tiles.take()))
            ao_t = [[], []]
            for bp in range(BLK):
                qk, free = (yield from gen.take())
                ht = [t for _, t in h]
                t_qk = (yield from mm(qk[:], [(h[kc][0][:, blk(bp)], w["w_qk"][:, kc, :]) for kc in range(KC)],
                          free, ht, ld("w_qk")))
                vb, free = (yield from gen.take())
                t_v = (yield from mms([(vb[64 * par:64 * par + 64, P * b:P * b + P],
                            [(h[kc][0][:, P * bp + T * b:P * bp + T * b + T],
                              w["w_v"][:, kc, :].rearrange("p (h two d) -> p two h d", two=2, d=HD)[:, par])
                             for kc in range(KC)]) for b in range(2) for par in range(2)],
                          free, ld("w_v")))
                vd, vfree = (yield from vbd.take())
                t_vd = []
                for par in range(2):
                    t_vd.append((yield from act.go(lambda e: e.activation(
                        vd[64 * par:64 * par + 64, :, :, par, :].rearrange("p b h d -> p (b h) d"),
                        vb[64 * par:64 * par + 64, 0:256].rearrange("p (x d) -> p x d", d=HD), ACT.Copy),
                        t_v, vfree, t_zero_v, cost=0.4)))
                gen.give(vb, t_vd)
                sq, free = (yield from tiles.take())
                t = (yield from act.go(lambda e: e.activation(sq[:], qk[:], ACT.Square), t_qk, free))
                ss, sfree = (yield from small.take())
                t = (yield from dve.go(lambda e: e.tensor_reduce(
                    ss[:, 0:32], sq[:].rearrange("p (h d) -> p h d", d=HD), AX, ALU.add), t, sfree))
                tiles.give(sq, t)
                t = (yield from dve.go(lambda e: e.tensor_scalar(ss[:, 0:32], ss[:, 0:32], 1.0 / HD, EPS_RMS,
                                                     ALU.mult, ALU.add), t))
                t = (yield from pool.go(lambda e: e.tensor_tensor(
                    ss[:, 32:64], ss[:, 0:32], neg_half.broadcast_to([P, 32]), ALU.pow), t, ld("cols"), cost=2.8))
                qkn, free = (yield from tiles.take())
                t = (yield from dve.go(lambda e: e.tensor_tensor(
                    qkn[:].rearrange("p (h d) -> p h d", d=HD), qk[:].rearrange("p (h d) -> p h d", d=HD),
                    ss[:, 32:64].unsqueeze(2).broadcast_to([P, 32, HD]), ALU.mult), t, free))
                gen.give(qk, t)
                small.give(ss, t)
                yield
                bank, free = (yield from gen.take())
                t = (yield from transposes([(bank[:, blk(i)], qkn[:, blk(i)]) for i in range(4)], t, free))
                tiles.give(qkn, t)
                qkt, free = (yield from tiles.take())
                t_qt = []
                for i in range(2):
                    t_qt.append((yield from act.go(lambda e: e.activation(
                        qkt[:, 256 * i:256 * i + 256], bank[:, 256 * i:256 * i + 256], ACT.Copy,
                        scale=w["qkn"][:, i:i + 1]), t, free, ld("qkn"), cost=0.5)))
                gen.give(bank, t_qt)
                scores, t_s = [], []
                for c in range(KC):
                    kd = []
                    for b in range(2):
                        kbd, free = (yield from tiles.take())
                        kd.append((kbd, (yield from pool.go(lambda e, o=kbd, c=c, b=b: e.tensor_tensor(
                            o[:].rearrange("p (h k) -> p h k", k=T),
                            qkt[:, 256 + P * c + T * b:256 + P * c + T * b + T].unsqueeze(1).broadcast_to([P, 8, T]),
                            w["head_mask"][:].unsqueeze(2).broadcast_to([P, 8, T]), ALU.mult),
                            t_qt, free, ld("head_mask"), cost=1.25))))
                    bank, free = (yield from gen.take())
                    t = (yield from mms([(bank[T * b:T * b + T, :],
                              [(qkt[:, P * c + T * b:P * c + T * b + T], kd[b][0][:])]) for b in range(2)],
                            free, t_qt, [t for _, t in kd]))
                    for x, _ in kd:
                        tiles.give(x, t)
                    sc, free = (yield from tiles.take())
                    scv = sc[:].rearrange("p (h k) -> p h k", k=T)
                    t_m = (yield from dve.go(lambda e, i=bank, o=scv: e.scalar_tensor_tensor(
                        o, i[:].rearrange("p (h k) -> p h k", k=T), HD ** -0.5,
                        w["causal"][:].unsqueeze(1).broadcast_to([P, 8, T]), ALU.mult, ALU.add),
                        t, free, ld("causal")))
                    gen.give(bank, t_m)
                    scores.append((sc, scv, t_m))
                    t_s.append(t)
                    yield
                tiles.give(qkt, t_s)
                st, sfree = (yield from small.take())
                probs = []
                for c, (sc, scv, t) in enumerate(scores):
                    m = st[:, 8 * c:8 * c + 8]
                    t = (yield from dve.go(lambda e, m=m, i=scv: e.tensor_reduce(m, i, AX, ALU.max), t, sfree))
                    t = (yield from pool.go(lambda e, m=m, i=scv: e.tensor_tensor(
                        i, i, m.unsqueeze(2).broadcast_to([P, 8, T]), ALU.subtract), t, cost=1.25))
                    t = (yield from act.go(lambda e, i=sc: e.activation(i[:], i[:], ACT.Exp), t))
                    t_sum = (yield from dve.go(lambda e, c=c, i=scv: e.tensor_reduce(
                        st[:, 16 + 8 * c:24 + 8 * c], i, AX, ALU.add), t))
                    bank, free = (yield from gen.take())
                    t = (yield from transposes([(bank[:, blk(i)], sc[:, blk(i)]) for i in range(4)], t, free))
                    tiles.give(sc, t, t_sum)
                    pt, free = (yield from tiles.take())
                    t_p = (yield from act.go(lambda e, o=pt, i=bank: e.activation(o[:], i[:], ACT.Copy), t, free))
                    gen.give(bank, t_p)
                    probs.append((pt, t_p))
                    sums = t_sum
                    yield
                t_r = (yield from dve.go(lambda e: e.reciprocal(st[:, 32:48], st[:, 16:32]), sums))
                ob, free = (yield from gen.take())
                t = (yield from mms([(ob[T * b:T * b + T, 32 * hp:32 * hp + 32],
                          [(probs[hp // 4][0][:, P * (hp % 4) + T * b:P * (hp % 4) + T * b + T],
                            vd[:, b, hp].rearrange("p two d -> p (two d)"))])
                         for hp in range(8) for b in range(2)], free, [t for _, t in probs], t_vd))
                vbd.give(vd, t)
                for x, _ in probs:
                    tiles.give(x, t)
                on, free = (yield from tiles.take())
                t = (yield from dve.go(lambda e: e.tensor_tensor(
                    on[:, 0:C].rearrange("p (h d) -> p h d", d=HD), ob[:, 0:C].rearrange("p (h d) -> p h d", d=HD),
                    st[:, 32:48].unsqueeze(2).broadcast_to([P, HEADS, HD]), ALU.mult), t, t_r, free))
                gen.give(ob, t)
                small.give(st, t)
                bank, free = (yield from gen.take())
                t = (yield from transposes([(bank[:, blk(i)], on[:, blk(i)]) for i in range(KC)], t, free))
                tiles.give(on, t)
                for kc in range(KC):
                    ao_t[kc].append((yield from act.go(lambda e, kc=kc, bp=bp: e.activation(
                        ao[kc][0][:, blk(bp)], bank[:, blk(kc)], ACT.Copy), t, ao[kc][1])))
                gen.give(bank, ao_t[0][-1], ao_t[1][-1])
                last_h = [t_qk, t_v]
                yield
            for x, _ in h:
                tiles.give(x, last_h)
            return [(ao[kc][0], ao_t[kc]) for kc in range(KC)]

        def top_two(xf):
            bank, free = (yield from gen.take())
            nb = BLK * EXPERTS
            t = (yield from mms([(bank[:, i * EXPERTS:(i + 1) * EXPERTS],
                      [(xf[kc][0][:, blk(i)], w["w_gate"][:, kc, :]) for kc in range(KC)])
                     for i in range(BLK)], free, [t for _, t in xf], ld("w_gate")))
            a, afree = (yield from small.take())
            d, dfree = (yield from small.take())
            f, ffree = (yield from small.take())
            pr, st, wt = a[:, 0:nb], a[:, 16:20], a[:, 32:32 + nb]

            def v(ap):
                return ap.rearrange("p (i e) -> p i e", e=EXPERTS)

            def per(ap):
                return ap.unsqueeze(2).broadcast_to([P, BLK, EXPERTS])
            t = (yield from dve.go(lambda e: e.tensor_scalar(pr, bank[:, 0:nb], FMAX, -FMAX, ALU.min, ALU.max), t, afree))
            gen.give(bank, t)
            t = (yield from dve.go(lambda e: e.tensor_reduce(st, v(pr), AX, ALU.max), t))
            t = (yield from dve.go(lambda e: e.tensor_tensor(v(pr), v(pr), per(st), ALU.subtract), t))
            t = (yield from act.go(lambda e: e.activation(pr, pr, ACT.Exp), t))
            t = (yield from dve.go(lambda e: e.tensor_reduce(st, v(pr), AX, ALU.add), t))
            t = (yield from dve.go(lambda e: e.reciprocal(st, st), t))
            t = (yield from dve.go(lambda e: e.tensor_tensor(v(pr), v(pr), per(st), ALU.mult), t))
            t_before = []
            for dst, free, op, which in ((d, dfree, ALU.is_ge, 0), (f, ffree, ALU.is_gt, 1)):
                for i in range(BLK):
                    one = pr[:, 4 * i:4 * i + 4]
                    t2 = (yield from dve.go(lambda e, dst=dst, i=i, one=one, op=op: e.tensor_tensor(
                        v(dst[:, 16 * i:16 * i + 16]), one.unsqueeze(1).broadcast_to([P, 4, 4]),
                        one.unsqueeze(2).broadcast_to([P, 4, 4]), op), t, free))
                    t_before.append(t2)
                t2 = (yield from dve.go(lambda e, dst=dst, which=which: e.tensor_tensor(
                    dst[:].rearrange("p (i m) -> p i m", m=16), dst[:].rearrange("p (i m) -> p i m", m=16),
                    w["rank"][:, which, :].unsqueeze(1).broadcast_to([P, BLK, 16]), ALU.mult),
                    t_before[-BLK:], ld("rank")))
                t_before.append(t2)
            t2 = (yield from dve.go(lambda e: e.tensor_tensor(d[:], d[:], f[:], ALU.add), t_before))
            small.give(f, t2)
            t2 = (yield from dve.go(lambda e: e.tensor_reduce(wt, d[:].rearrange("p (m j) -> p m j", j=4), AX, ALU.add), t2))
            small.give(d, t2)
            t = (yield from dve.go(lambda e: e.scalar_tensor_tensor(wt, wt, TOPK - 0.5, pr, ALU.is_lt, ALU.mult), t2))
            t = (yield from dve.go(lambda e: e.tensor_reduce(st, v(wt), AX, ALU.add), t))
            t = (yield from dve.go(lambda e: e.tensor_scalar(st, st, EPS_TOP, None, ALU.add), t))
            t = (yield from dve.go(lambda e: e.reciprocal(st, st), t))
            t = (yield from dve.go(lambda e: e.tensor_tensor(v(wt), v(wt), per(st), ALU.mult), t))
            return a, wt, t

        def middle(g):
            while ("scan", g) not in handed:
                yield WAIT
            inputs, t_scan, t_coef = handed.pop(("scan", g))
            X, tiles = inputs[0], mid_tiles[g % 2]
            xt = []
            s = sem(f"ldx_mid{g}")
            for kc in range(KC):
                tile, free = (yield from tiles.take())
                xt.append((tile, sp.dma(s, 16 * KC, lambda e: e.dma_start(tile[:], dram["xT"][kc, :, g, :]), free)))
            t_z = []
            for c in range(IC):
                bank, free = (yield from gen.take())
                t = (yield from mm(bank[:], [(w["w_in"][:, kc, DI + P * c:DI + P * c + P], xt[kc][0][:]) for kc in range(KC)],
                       free, [t for _, t in xt], ld("w_in")))
                sg, sfree = (yield from tiles.take())
                t_sg = (yield from act.go(lambda e: e.activation(sg[:], bank[:], ACT.Silu), t, sfree))
                gen.give(bank, t_sg)
                t_z.append((yield from pool.go(lambda e, c=c, i=sg: e.tensor_tensor(X[:, c, :], X[:, c, :], i[:], ALU.mult),
                                   t_sg, t_scan, cost=1.3)))
                tiles.give(sg, t_z[-1])
                yield
            for tile, _ in xt:
                tiles.give(tile, t)
            x1 = []
            for m in range(KC):
                bank, free = (yield from gen.take())
                t = yield from long_mm(bank[:], [(w["w_out"][:, c, blk(m)], X[:, c, :]) for c in range(IC)],
                       free, t_z, ld("w_out"))
                tile, tfree = (yield from tiles.take())
                t_x = (yield from act.go(lambda e, o=tile, i=bank: e.activation(
                    o[:].rearrange("p (b t) -> p t b", t=T), t_major(i[:]), ACT.Copy), t, tfree))
                gen.give(bank, t_x)
                x1.append((tile, t_x))
                yield
            scan_inputs.give(inputs, t, t_coef)
            h = yield from rms_norm(tiles, x1, 0)
            yield
            ao = yield from attention(tiles, h)
            for m in range(KC):
                bank, free = (yield from gen.take())
                lo = KEPT if m == 0 else 0
                t = (yield from mm(bank[lo:, :], [(w["w_o"][:, kc, P * m + lo:P * m + P], ao[kc][0][:]) for kc in range(KC)],
                       free, [t for _, t in ao], ld("w_o")))
                t_x = (yield from dve.go(lambda e, o=x1[m][0], i=bank, lo=lo: e.tensor_tensor(
                    o[lo:, :], o[lo:, :], i[lo:, :], ALU.add), t, x1[m][1], [t for _, t in h]))
                gen.give(bank, t_x)
                x1[m] = (x1[m][0], [t_x, x1[m][1]])
            for tile, _ in ao:
                tiles.give(tile, t)
            yield
            xf = yield from rms_norm(tiles, x1, 1)
            acc, free_acc = yield from accs.take()
            t_acc = [sp.dma(sem(f"ld_acc{g}"), 16, lambda e: e.dma_start(
                acc[:], dram["x"][g * TOK:(g + 1) * TOK, :].rearrange("(i p) c -> p i c", p=P)), free_acc)]
            yield
            for i2 in range(2):
                bank, free = (yield from gen.take())
                t = (yield from transposes([(bank[:, P * (2 * j + kc):P * (2 * j + kc) + P], x1[kc][0][:, blk(2 * i2 + j)])
                                for j in range(2) for kc in range(KC)], free, x1[0][1], x1[1][1]))
                t_a = (yield from dve.go(lambda e, i2=i2, i=bank: e.tensor_tensor(
                    acc[:, 2 * i2:2 * i2 + 2, :], acc[:, 2 * i2:2 * i2 + 2, :],
                    i[:].rearrange("p (i c) -> p i c", c=C), ALU.add), t, t_acc[0]))
                gen.give(bank, t_a)
                t_acc.append(t_a)
            for tile, _ in x1:
                tiles.give(tile, t, [t for _, t in xf])
            yield
            route, wt, t_wt = yield from top_two(xf)
            handed["middle", g] = (xf, acc, [t_acc[1], t_acc[1], t_acc[2], t_acc[2]], route, wt, t_wt)
            yield

        def experts(g):
            while ("middle", g) not in handed:
                yield WAIT
            xf, acc, last_add, route, wt, t_wt = handed.pop(("middle", g))
            take = hidden_tiles

            def expert(index, hidden, weight):
                wc, t_w, bufs = yield from weight_of(weight)
                for i2 in range(2):
                    bank, free = (yield from gen.take())
                    t = (yield from mms([(bank[:, MOD * j:MOD * j + MOD],
                              [(x[:, blk(2 * i2 + j)], wc[c]) for c, (x, _) in enumerate(hidden)])
                             for j in range(2)], free, [t for _, t in hidden], t_w))
                    t_a = []
                    for j in range(2):
                        i = 2 * i2 + j
                        last_add[i] = (yield from dve.go(lambda e, i=i, j=j, ps=bank: e.scalar_tensor_tensor(
                            acc[:, i, KEPT:], ps[:, MOD * j:MOD * j + MOD],
                            wt[:, EXPERTS * i + index:EXPERTS * i + index + 1], acc[:, i, KEPT:],
                            ALU.mult, ALU.add), t, t_wt, last_add[i]))
                        t_a.append(last_add[i])
                    gen.give(bank, t_a)
                    yield
                drop(take, hidden, t)
                drop_weight(bufs, t)

            hid, t = yield from dense(take, xf, "e1_w1", IC, ACT.Silu)
            gated = []
            wc, t_w, bufs = yield from weight_of("e1_w2")
            for m in range(IC):
                bank, free = (yield from gen.take())
                t_m = (yield from mm(bank[:], [(wc[kc][:, blk(m)], xf[kc][0][:]) for kc in range(KC)], free, t_w))
                t = (yield from dve.go(lambda e, o=hid[m][0], i=bank: e.tensor_tensor(o[:], o[:], i[:], ALU.mult), t_m, hid[m][1]))
                gen.give(bank, t)
                gated.append((hid[m][0], t))
                yield
            drop_weight(bufs, t_m)
            yield from expert(1, gated, "e1_down")
            hid, t = yield from dense(take, xf, "e0_up", IC, ACT.Gelu)
            yield from expert(0, hid, "e0_down")
            hid, t = yield from dense(take, xf, "e2_l1", IC, ACT.Gelu)
            for weight in ("e2_l2", "e2_l3"):
                nxt, t = yield from dense(take, hid, weight, IC, ACT.Gelu)
                drop(take, hid, t)
                hid = nxt
            yield from expert(2, hid, "e2_l4")
            low, t = yield from dense(take, xf, "e3_down", KC, ACT.Gelu)
            drop(mid_tiles[g % 2], xf, t)
            hid, t = yield from dense(take, low, "e3_up", IC, ACT.Gelu)
            drop(take, low, t)
            yield from expert(3, hid, "e3_out")
            small.give(route, last_add)
            s_out = sem("stores")
            accs.give(acc, sp.dma(s_out, 16 * (g + 1), lambda e: e.dma_start(
                out[g * TOK:(g + 1) * TOK, :].rearrange("(i p) c -> p i c", p=P), acc[:]), last_add))

        def every_group(name, stage, groups=range(GROUPS)):
            for g in groups:
                steps = stage(g)
                while True:
                    for lane in lanes:
                        lane.phase(f"{name}{g // 2}")
                    try:
                        said = next(steps)
                    except StopIteration:
                        break
                    if said is not None:
                        yield said

        stages = [every_group("w", expert_weights), every_group("scan", scan), every_group("front", front),
                  every_group("mid0_", middle, range(0, GROUPS, 2)),
                  every_group("mid1_", middle, range(1, GROUPS, 2)), every_group("exp", experts)]
        coming = {n: (sp, 0.0) for n in range(len(stages))}
        while coming:
            def start(n):
                lane, due = coming[n]
                return max(lane.clock, due)
            free_to_go = sorted((n for n in coming if coming[n] != WAIT), key=lambda n: (start(n), n))
            blocked = [n for n in coming if coming[n] == WAIT]
            moved = False
            for n in blocked + free_to_go[:1]:
                was = coming[n]
                try:
                    coming[n] = next(stages[n])
                except StopIteration:
                    del coming[n]
                    moved = True
                    continue
                moved = moved or coming[n] != WAIT or was != WAIT
            assert moved, "the stages wait for one another"

        sp.wait(Tick(sem("stores"), 16 * GROUPS, 0.0))


def chunked(a, parts):
    return np.ascontiguousarray(a.reshape(parts, P, -1).transpose(1, 0, 2))


def lay_weights(v):
    c, f = (lambda n: v["L0_cond_" + n]), (lambda n: v["L0_ffn_" + n])
    d = {}
    d["w_in"] = chunked(c("W_in").T, KC)
    wx = c("W_xproj").T
    d["w_xb"] = chunked(wx[:, 0:NS], IC)
    gap = np.zeros((DI, NS), wx.dtype)
    d["w_xcd"] = chunked(np.concatenate([wx[:, NS:2 * NS], gap, wx[:, 2 * NS:]], 1), IC)
    d["w_out"] = chunked(c("W_out").T, IC)
    d["w_qk"] = chunked(np.concatenate([f("wq").T, f("wk").T], 1), KC)
    for name, key, n in (("w_v", "wv", KC), ("w_o", "wo", KC), ("w_gate", "gate_w", KC), ("e0_up", "e0_up", KC),
                         ("e1_w1", "e1_w1", KC), ("e1_w2", "e1_w2", KC), ("e2_l1", "e2_l1", KC),
                         ("e2_l2", "e2_l2", IC), ("e2_l3", "e2_l3", IC), ("e3_down", "e3_down", KC),
                         ("e3_up", "e3_up", KC)):
        d[name] = chunked(f(key).T, n)
    for name in ("e0_down", "e1_down", "e2_l4", "e3_out"):
        d[name] = chunked(f(name).T[:, KEPT:], IC)
    d["temb"] = chunked(v["cond_2048"].T, IC)
    d["w_conv"] = chunked(c("W_conv").reshape(DI, NCONV), IC)
    d["vecs"] = np.ascontiguousarray(np.stack(
        [c(n).reshape(IC, P).T for n in ("b_conv", "ln_g", "ln_b", "D")], 1))
    d["norms"] = np.ascontiguousarray(np.stack([f(n).reshape(KC, P).T for n in ("n1_w", "n2_w")], 2))
    d["qkn"] = np.ascontiguousarray(np.stack([np.tile(f(n), P // HD) for n in ("qn_w", "kn_w")], 1))
    dt_w = np.zeros((P, NS + 2), wx.dtype)
    dt_w[32:48, 0:NS] = c("W_dt").T
    dt_w[32:48, NS] = c("b_dt")
    dt_w[32:48, NS + 1] = c("A_log")
    d["dt_w"] = dt_w
    return d


def lay_constants():
    d, i = {}, np.arange(P)
    d["ident"] = np.eye(P)
    d["sel"] = (i[:, None, None] == 32 * np.arange(BLK)[None, :, None] + (i % 32)[None, None, :])
    d["mean_mat"] = np.full((P, P), 1.0 / DI)
    d["cols"] = np.tile([1.0 / DI, 1.0 / C, 1.0, -0.5, 0.5], (P, 1))
    d["wu_mask"] = (i % 32)[:, None] == np.arange(32)[None, :]
    d["c_mask"] = (i // NS)[:, None] == np.arange(GB)[None, :]
    d["causal"] = np.where(np.arange(T)[None, :] <= (i % T)[:, None], 0.0, MASKED)
    d["head_mask"] = (i // HD)[:, None] == np.arange(8)[None, :]
    e = np.arange(EXPERTS)
    lower = (e[None, :] < e[:, None]).reshape(-1)
    upper = (e[None, :] > e[:, None]).reshape(-1)
    d["rank"] = np.tile(np.stack([lower, upper])[None], (P, 1, 1))
    return {k: np.ascontiguousarray(a.astype(np.float32)) for k, a in d.items()}


def kernel(**inputs):
    import concourse.bacc as bacc
    from concourse.bass_utils import run_bass_kernel_spmd

    v = {k: np.asarray(a) for k, a in inputs.items()}
    arrays = {**lay_weights(v), **lay_constants()}
    x = v["x"]
    arrays["xT"] = np.ascontiguousarray(
        x.reshape(GROUPS, GB, T, KC, P).transpose(3, 4, 0, 2, 1).reshape(KC, P, GROUPS, TOK))
    arrays["x"] = np.ascontiguousarray(x.reshape(B * T, C))
    for k, s in {**W_SHAPES, **EXPERT_SHAPES}.items():
        assert arrays[k].shape == (P,) + s, (k, arrays[k].shape)

    nc = bacc.Bacc("TRN2", target_bir_lowering=False, num_devices=1)
    dram = {k: nc.dram_tensor(f"in_{k}", a.shape, mybir.dt.from_np(a.dtype), kind="ExternalInput").ap()
            for k, a in arrays.items()}
    out = nc.dram_tensor("out_y", (B * T, C), F32, kind="ExternalOutput").ap()
    build_program(nc, dram, out)
    r = run_bass_kernel_spmd(nc, [{f"in_{k}": a for k, a in arrays.items()}], core_ids=[0])
    return r.results[0]["out_y"].reshape(B, T, C)
```

```python
from collections import namedtuple
from contextlib import ExitStack

import numpy as np

import concourse.bass as bass
from concourse import mybir

F32 = mybir.dt.float32
F32R = mybir.dt.float32r
ACT = mybir.ActivationFunctionType
ALU = mybir.AluOpType
AX = mybir.AxisListType.X

P = 128
B, T, C = 64, 64, 256
DI = 512
NS = 16
GROUPS = 8
GB = B // GROUPS
TOK = GB * T
KC, IC = C // P, DI // P
BLK = TOK // P
HEADS, HD = 16, 16
VW = 2 * HD + 2
EXPERTS, TOPK = 4, 2
KEPT = 64
MOD = C - KEPT
STEPS_X = 4
NX = T // STEPS_X
U_BANKS = 2
WRING = 5
HIDDEN = 8
MIDS, MID_TILES = 2, 9
PIECE = 2
RING_H = 6
FROM_PE, TO_PE, HOP, OWN = 0.6, 0.7, 0.6, 0.6
DMA_LATENCY, TABLE_LOAD, TINY = 2.5, 1.3, 0.09
USUAL = {"pe": 0.85, "act": 0.49, "dve": 0.6, "pool": 1.0, "sp": 0.0}
XN = 3
EAGER, EAGER_FIRST, FIRST = 0.1, 0.1, 3
CLIP = 10.0
EPS_LN, EPS_RMS, EPS_TOP = 1e-5, 1.1920929e-07, 1e-8
MASKED = -1.0e30
FMAX = 3.4028234663852886e38
NCONV = 4

W_SHAPES = {
    "w_xr": (KC, DI), "w_z": (KC, DI), "w_x": (IC, 80), "w_out": (IC, C),
    "w_qk": (KC, 2 * C), "w_v": (KC, C), "w_o": (KC, C), "w_gate": (KC, EXPERTS),
    "temb": (IC, B), "w_conv": (IC, NCONV), "vecs": (4, IC), "norms": (KC, 2), "qkn": (2,),
    "dt_w": (NS + 2,),
    "ident": (P,), "sel": (BLK, P), "mean_mat": (P,), "cols": (5,), "wu_mask": (32,),
    "c_mask": (GB,), "causal": (T,), "head_mask": (8,), "rank": (2, EXPERTS * EXPERTS),
}
EXPERT_SHAPES = {
    "e1_w1": (KC, DI), "e1_w2": (KC, DI), "e2_l1": (KC, DI), "e1_down": (IC, MOD), "e2_l2": (IC, DI),
    "e2_l3": (IC, DI), "e0_up": (KC, DI), "e2_l4": (IC, MOD), "e3_down": (KC, C), "e0_down": (IC, MOD),
    "e3_up": (KC, DI), "e3_out": (IC, MOD),
}
WSLOT = KC * DI
LOADS = [("w_xr", "temb"), ("w_conv", "vecs", "mean_mat", "cols", "ident"),
         ("w_x", "dt_w", "sel", "wu_mask", "c_mask"),
         ("w_z", "w_out", "norms", "w_qk", "w_v", "qkn", "head_mask", "causal", "w_o", "w_gate", "rank")]


Tick = namedtuple("Tick", "sem count at by", defaults=(None,))
WAIT = "blocked"
TABLE = {ACT.Silu: "silu", ACT.Gelu: "gelu"}


class Lane:

    def __init__(self, name, engine, new_sem):
        self.name, self.engine, self.new_sem, self.counts, self.seen = name, engine, new_sem, {}, {}
        self.clock, self.table, self.usual = 0.0, None, USUAL[name]
        self.phase("setup")

    def phase(self, stage):
        self.key = f"{self.name}_{stage}"

    def wait(self, *after):
        for tick in flat(after):
            if self.seen.get(id(tick.sem), 0) < tick.count:
                self.engine.wait_ge(tick.sem, tick.count)
                self.seen[id(tick.sem)] = tick.count
            self.clock = max(self.clock, self.sees(tick))

    def sees(self, tick):
        if tick.by is None:
            return tick.at
        if tick.by is self:
            return tick.at + (0.0 if self.name == "pe" else OWN)
        return tick.at + (FROM_PE if tick.by.name == "pe" else TO_PE if self.name == "pe" else HOP)

    def do(self, build, *after, cost=None, table=None):
        self.wait(after)
        self.clock += (self.usual if cost is None else cost) + self.switch(table)
        self.table = table or self.table
        n = self.counts[self.key] = self.counts.get(self.key, 0) + 1
        sem = self.new_sem(self.key)
        build(self.engine).then_inc(sem, 1)
        return Tick(sem, n, self.clock, self)

    def switch(self, table):
        return TABLE_LOAD if table and table != self.table else 0.0

    def go(self, build, *after, cost=None, table=None):
        yield self, max([self.sees(t) for t in flat(after)], default=0.0), table
        return self.do(build, *after, cost=cost, table=table)

    def dma(self, sem, total, build, *after):
        self.wait(after)
        build(self.engine).then_inc(sem, 16)
        return Tick(sem, total, self.clock + DMA_LATENCY)


def flat(ticks):
    if ticks is None:
        return []
    if isinstance(ticks, Tick):
        return [ticks]
    return [t for part in ticks for t in flat(part)]


class Slots:

    def __init__(self, bufs):
        self.bufs = [(b, []) for b in bufs]

    def take(self):
        while not self.bufs:
            yield WAIT
        first = min(range(len(self.bufs)), key=lambda i: max([t.at for t in self.bufs[i][1]], default=0))
        return self.bufs.pop(first)

    def give(self, buf, *last_readers):
        self.bufs.append((buf, flat(last_readers)))


def build_program(nc, dram, out):
    ctx = ExitStack()
    with ctx:
        def sb(name, shape, dt=F32):
            return ctx.enter_context(nc.sbuf_tensor(name, list(shape), dt))

        sems = {}

        def sem(name):
            if name not in sems:
                sems[name] = ctx.enter_context(nc.semaphore(name))
            return sems[name]

        pe, act, dve, pool, sp = (Lane(n, e, sem) for n, e in (
            ("pe", nc.tensor), ("act", nc.scalar), ("dve", nc.vector), ("pool", nc.gpsimd), ("sp", nc.sync)))
        lanes = (pe, act, dve, pool)

        w = {k: sb(k, (P,) + s) for k, s in W_SHAPES.items()}
        front_tiles = Slots([sb(f"front{i}", (P, 512)) for i in range(5)])
        loaded = {}
        handed = {}

        def load_x(g, stage, tiles):
            xt, s = [], sem(f"ldx_{stage}{g}")
            for kc in range(KC):
                tile, free = (yield from tiles.take())
                xt.append((tile, sp.dma(s, 16 * KC, lambda e: e.dma_start(tile[:], dram["xT"][kc, :, g, :]), free)))
            return xt

        def load_weights():
            for n, batch in enumerate(LOADS):
                for k in batch:
                    loaded[k] = sp.dma(sem(f"weights{n}"), 16 * len(batch), lambda e: e.dma_start(w[k][:], dram[k]))
                if n == 0:
                    first_x = yield from load_x(0, "front", front_tiles)
            handed["x", 0] = first_x

        def ld(*names):
            return [loaded[n] for n in names]

        ident, cols = w["ident"], w["cols"]
        col_ln, col_rms, col_one = cols[:, 0:1], cols[:, 1:2], cols[:, 2:3]
        neg_half, half = cols[:, 3:4], cols[:, 4:5]
        ident_r = sb("ident_r", (P, P), F32R)
        na = sb("na", (P, 2))

        scan_inputs = Slots([(sb(f"xn{i}", (P, IC, TOK)), sb(f"ad{i}", (P, T)), sb(f"cc{i}", (P, T)),
                              sb(f"b4{i}", (P, NX, NS))) for i in range(XN)])
        xr_pad = [sb(f"xr_pad{i}", (P, (T + NCONV - 1) * GB)) for i in range(2)]
        xr_slots = Slots(xr_pad)
        mid_tiles = [Slots([sb(f"mid{j}_{i}", (P, 512)) for i in range(MID_TILES)]) for j in range(MIDS)]
        half_tiles = Slots([sb(f"half{i}", (P, 512)) for i in range(6)])
        wring = Slots([sb(f"wring{i}", (P, WSLOT)) for i in range(WRING)])
        hidden_tiles = Slots([sb(f"hidden{i}", (P, 512)) for i in range(HIDDEN)])
        small = Slots([sb(f"small{i}", (P, 64)) for i in range(8)])
        accs = Slots([sb(f"acc{i}", (P, BLK, C)) for i in range(2)])
        vbds = [sb(f"vbd{i}", (P, 2, HEADS // 2, VW)) for i in range(3)]
        vbd = Slots(vbds)
        cd_packs = Slots([sb("cd_pack", (48, GB, T))])

        xqs = Slots([sb("xq", (P, IC, 2, 2, 32), F32R)])
        xrows = Slots([sb(f"xrow{i}", (P, DI), F32R) for i in range(2)])
        wus = Slots([sb(f"wu{i}", (P, 32, NS), F32R) for i in range(2)])
        hs = Slots([sb(f"h{i}", (P, DI)) for i in range(RING_H)])
        ytoks = Slots([sb("ytok", (P, DI))])
        cdiag_bufs = [sb(f"cdiag{i}", (P, 16, 32)) for i in range(2)]
        cdiags = Slots(cdiag_bufs)

        banks = [ctx.enter_context(nc.psum_tensor(f"bank{i}", [P, 512], F32)) for i in range(8)]
        us, ys, gen = Slots(banks[0:U_BANKS]), Slots(banks[U_BANKS:U_BANKS + 1]), Slots(banks[U_BANKS + 1:])

        for _ in load_weights():
            assert False, "the first tiles are free"
        t_identr = dve.do(lambda e: e.tensor_copy(ident_r[:], ident[:]), ld("ident"))
        zeroed = [dve.do(lambda e, x=x: e.memset(x[:, 0:(NCONV - 1) * GB], 0.0)) for x in xr_pad]
        t_zero_cd = [dve.do(lambda e, x=x: e.memset(x[:], 0.0)) for x in cdiag_bufs]
        t_zero_v = [pool.do(lambda e, x=x: e.memset(x[:], 0.0)) for x in vbds]
        t_zero_v = [dve.do(lambda e, x=x, par=par: e.memset(
            x[64 * par:64 * par + 64, :, :, 2 * HD + par:2 * HD + par + 1], 1.0), t_zero_v, cost=TINY)
            for x in vbds for par in range(2)]
        t_na = act.do(lambda e: e.activation(na[32:48, 0:1], w["dt_w"][32:48, NS + 1:NS + 2], ACT.Tanh),
                      ld("dt_w"))
        t_na = dve.do(lambda e: e.tensor_scalar(na[32:48, 1:2], na[32:48, 0:1], -0.01, None, ALU.mult),
                      t_na)

        def mm(out_ap, pairs, *after):
            return (yield from mms([(out_ap, pairs)], *after))

        def accumulate(out_ap, pairs, first, last, *after):
            for i0 in range(0, len(pairs), PIECE):
                part = pairs[i0:i0 + PIECE]

                def go(e):
                    for i, (lhs, rhs) in enumerate(part, i0):
                        ins = e.matmul(out_ap, lhs, rhs, start=first and i == 0, stop=last and i == len(pairs) - 1)
                    return ins
                t = (yield from pe.go(go, *after, cost=sum(matmul_cost(*pair) for pair in part)))
            return t

        def matmul_cost(lhs, rhs):
            n, m = (int(np.prod(ap.shape[1:])) for ap in (rhs, lhs))
            one_pass = rhs.dtype == F32R
            cost = max(n * (1 if one_pass else 4) / 2400, 0.06 if one_pass else 0.21)
            return cost * (0.6 if m == 64 else 1) + (0.03 if one_pass else 0)

        def mms(jobs, *after):
            jobs = [(o, list(ps)) for o, ps in jobs]

            def go(e):
                for o, ps in jobs:
                    for i, (lhs, rhs) in enumerate(ps):
                        last = e.matmul(o, lhs, rhs, start=i == 0, stop=i == len(ps) - 1)
                return last
            return (yield from pe.go(go, *after, cost=sum(matmul_cost(*pair) for _, ps in jobs for pair in ps)))

        def transposes(jobs, *after, identity=ident[:]):
            def go(e):
                for o, i in jobs:
                    last = e.transpose(o, i, identity)
                return last
            return (yield from pe.go(go, after, ld("ident"), cost=0.13 * len(jobs)))

        def blk(i):
            return slice(i * P, (i + 1) * P)

        def token_sums(tiles, chunks, column):
            total, t_total = None, None
            for x, t in chunks:
                sq, free = (yield from tiles.take())
                t = (yield from act.go(lambda e: e.activation(sq[:], x, ACT.Square), free, t))
                if total is None:
                    total, t_total = sq, t
                    continue
                t_total = (yield from sooner(((dve, 0.6), (pool, 1.23)), lambda e: e.tensor_tensor(
                    total[:], total[:], sq[:], ALU.add), t_total, t))
                tiles.give(sq, t_total)
            bank, free = (yield from gen.take())
            t = (yield from mms([(bank[:, i:i + 1], [(total[:, blk(i)], column)]) for i in range(BLK)],
                    free, t_total, ld("cols")))
            tiles.give(total, t)
            return bank, t

        def sooner(choices, build, *after):
            lane, cost = min(choices, key=lambda c: max([c[0].clock] + [c[0].sees(t) for t in flat(after)]) + c[1])
            return (yield from lane.go(build, *after, cost=cost))

        def over_tokens(r, t_r):
            bank, free = (yield from gen.take())
            t = (yield from mms([(bank[:, blk(i)], [(r[:, i:i + 1].broadcast_to([P, P]), ident[:])])
                     for i in range(BLK)], free, t_r, ld("ident")))
            return bank, t

        def rsqrt_of(bank, t_bank, eps):
            s, free = (yield from small.take())
            t = (yield from dve.go(lambda e: e.tensor_scalar(s[:, 0:BLK], bank[:, 0:BLK], eps, None, ALU.add),
                       free, t_bank, cost=TINY))
            gen.give(bank, t)
            t = (yield from pool.go(lambda e: e.tensor_tensor(s[:, 8:8 + BLK], s[:, 0:BLK],
                                                  neg_half.broadcast_to([P, BLK]), ALU.pow), t, ld("cols"), cost=0.97))
            return s, t

        def t_major(ap):
            return ap.rearrange("p (t b) -> p t b", b=GB)

        def front(g):
            (X, decay, c_rows, b4), x_free = yield from scan_inputs.take()
            xt = handed.pop(("x", g), None) or (yield from load_x(g, "front", front_tiles))
            t_silu = []
            for c in range(IC):
                bank, free = (yield from gen.take())
                t = (yield from mm(bank[:], [(w["w_xr"][:, kc, blk(c)], xt[kc][0][:]) for kc in range(KC)],
                       free, [t for _, t in xt], ld("w_xr")))
                if c == IC - 1:
                    for tile, _ in xt:
                        front_tiles.give(tile, t)
                pad, pfree = (yield from xr_slots.take())
                body = pad[:, (NCONV - 1) * GB:]
                t = (yield from dve.go(lambda e, o=body, i=bank, c=c: e.tensor_tensor(
                    t_major(o), t_major(i[:]),
                    w["temb"][:, c, g * GB:(g + 1) * GB].unsqueeze(1).broadcast_to([P, T, GB]), ALU.add),
                    t, pfree, zeroed, ld("temb")))
                gen.give(bank, t)
                t = (yield from act.go(lambda e, i=body, c=c: e.activation(
                    X[:, c, :], i, ACT.Identity, scale=w["w_conv"][:, c, NCONV - 1:NCONV],
                    bias=w["vecs"][:, 0, c:c + 1]), t, x_free, ld("w_conv", "vecs")))
                for k in range(NCONV - 1):
                    t = (yield from dve.go(lambda e, i=pad, c=c, k=k: e.scalar_tensor_tensor(
                        X[:, c, :], i[:, k * GB:k * GB + TOK], w["w_conv"][:, c, k:k + 1], X[:, c, :],
                        ALU.mult, ALU.add), t))
                xr_slots.give(pad, t)
                t_silu.append((yield from act.go(lambda e, c=c: e.activation(X[:, c, :], X[:, c, :], ACT.Silu), t, table="silu")))
            total, free = (yield from front_tiles.take())
            t = free
            for c in range(1, IC):
                t = (yield from sooner(((dve, 0.6), (pool, 1.23)), lambda e: e.tensor_tensor(
                    total[:], X[:, 0, :] if c == 1 else total[:], X[:, c, :], ALU.add), t, t_silu[0], t_silu[c]))
            bank, free = (yield from gen.take())
            t = (yield from mm(bank[:], [(w["mean_mat"][:], total[:])], free, t, ld("mean_mat")))
            front_tiles.give(total, t)
            t_c = []
            for c in range(IC):
                t_c.append((yield from dve.go(lambda e: e.tensor_tensor(X[:, c, :], X[:, c, :], bank[:], ALU.subtract), t)))
            gen.give(bank, t_c)
            bank, t = (yield from token_sums(front_tiles, [(X[:, c, :], t_c[c]) for c in range(IC)], col_ln))
            r, t = yield from rsqrt_of(bank, t, EPS_LN)
            bank, t = yield from over_tokens(r[:, 8:8 + BLK], t)
            small.give(r, t)
            t_c, t_x = [], []
            for c in range(IC):
                t_c.append((yield from dve.go(lambda e: e.scalar_tensor_tensor(
                    X[:, c, :], X[:, c, :], w["vecs"][:, 1, c:c + 1], bank[:], ALU.mult, ALU.mult), t)))
                t_x.append((yield from act.go(lambda e: e.activation(
                    X[:, c, :], X[:, c, :], ACT.Identity, bias=w["vecs"][:, 2, c:c + 1]), t_c[c])))
            gen.give(bank, t_c)
            bank, t = (yield from token_sums(front_tiles, [(X[:, c, :], t_x[c]) for c in range(IC)], col_one))
            nrm, free = (yield from small.take())
            t = (yield from dve.go(lambda e, o=nrm, i=bank: e.tensor_scalar(o[:, 0:BLK], i[:, 0:BLK], 1.0, None, ALU.min),
                       free, t, cost=TINY))
            gen.give(bank, t)
            t_n = (yield from pool.go(lambda e, o=nrm: e.tensor_tensor(
                o[:, 8:8 + BLK], o[:, 0:BLK], half.broadcast_to([P, BLK]), ALU.pow), t, cost=0.97))
            bank, free = (yield from gen.take())
            t = (yield from mm(bank[0:80, :], [(w["w_x"][:, c, :], X[:, c, :]) for c in range(IC)], free, t_x, ld("w_x")))
            dt_tile, free = (yield from front_tiles.take())
            cd_pack, cd_free = yield from cd_packs.take()
            t_b = (yield from act.go(lambda e, i=bank: e.activation(dt_tile[64:80, :], i[64:80, :], ACT.Copy), t, free))
            t_dt = (yield from act.go(lambda e, i=bank: e.activation(dt_tile[32:48, :], i[32:48, :], ACT.Copy), t, free))
            t_cp = (yield from act.go(lambda e, i=bank: e.activation(
                cd_pack[0:NS].rearrange("p b t -> p t b"), t_major(i[0:NS, :]), ACT.Copy), t, cd_free))
            gen.give(bank, t_b, t_dt, t_cp)
            bank, free = (yield from gen.take())
            t = t_b = (yield from transposes([(bank[:, i * NS:(i + 1) * NS], dt_tile[64:80, blk(i)]) for i in range(BLK)],
                                             free, t_b, identity=ident[64:80, 64:80]))
            bt, free = (yield from small.take())
            t = (yield from dve.go(lambda e, o=bt, i=bank, n=nrm: e.tensor_tensor(
                o[:].rearrange("p (i n) -> p i n", n=NS), i[:, 0:BLK * NS].rearrange("p (i n) -> p i n", n=NS),
                n[:, 8:8 + BLK].unsqueeze(2).broadcast_to([P, BLK, NS]), ALU.mult), free, t, t_n, cost=0.14))
            gen.give(bank, t)
            small.give(nrm, t)
            bank, free = (yield from gen.take())
            t = (yield from mms([(bank[:, i * 64:(i + 1) * 64], [(w["sel"][:, i, :], bt[:])]) for i in range(BLK)],
                    free, t, ld("sel")))
            small.give(bt, t)
            tile, free = (yield from front_tiles.take())
            hi = tile[:, 0:256]
            t = (yield from dve.go(lambda e, o=hi, i=bank: e.tensor_copy(o.bitcast(F32R), i[:, 0:256]), free, t))
            b4v = b4[:].rearrange("p (k s) n -> p s k n", s=4)

            def rows(ap, a, z):
                return ap[a:z].rearrange("p (s k n) -> p s k n", s=4, n=NS)
            t1 = (yield from dve.go(lambda e, i=hi: e.tensor_copy(b4v[0:64], rows(i, 0, 64)), t, x_free, cost=0.2))
            t2 = (yield from dve.go(lambda e, i=hi, ps=bank: e.tensor_tensor(
                b4v[64:P], rows(ps[:, 0:256], 64, P), rows(i, 64, P), ALU.subtract), t, x_free))
            gen.give(bank, t1, t2)
            front_tiles.give(tile, t1, t2)
            bank, free = (yield from gen.take())
            t = (yield from mm(bank[32:48, :], [(w["dt_w"][32:48, 0:NS], dt_tile[32:48, :])], free, t_dt, ld("dt_w")))
            t = (yield from act.go(lambda e, o=dt_tile, i=bank: e.activation(
                o[32:48, :], i[32:48, :], ACT.Tanh, bias=w["dt_w"][32:48, NS:NS + 1]), t))
            gen.give(bank, t)
            t = (yield from dve.go(lambda e, i=dt_tile: e.tensor_scalar(
                cd_pack[32:48].rearrange("p b t -> p t b"), t_major(i[32:48, :]), na[32:48, 1:2], 1.0,
                ALU.mult, ALU.add), t, t_na, cd_free))
            front_tiles.give(dt_tile, t, t_b)
            s = sem(f"coef{g}")
            for b in range(GB):
                t_coef = sp.dma(s, 32 * GB, lambda e: e.dma_start(
                    c_rows[b * NS:(b + 1) * NS, :], cd_pack[0:NS, b, :]), t_cp, x_free)
                t_coef = sp.dma(s, 32 * GB, lambda e: e.dma_start(
                    decay[b * NS:(b + 1) * NS, :], cd_pack[32:48, b, :]), t, x_free)
            cd_packs.give(cd_pack, t_coef)
            handed["front", g] = ((X, decay, c_rows, b4), [t_x, t1, t2, t_coef])

        laid_out, brought, stepped = [], [], []

        def lay_out(g):
            while ("front", g) not in handed:
                yield WAIT
            inputs, t_in = handed.pop(("front", g))
            X, decay, c_rows, b4 = inputs
            handed["scan inputs", g] = (inputs, t_in)
            for k in range(NX):
                q, qfree = yield from xqs.take()
                src = X[:, :, 32 * k:32 * k + 32].unsqueeze(2).broadcast_to([P, IC, 2, 32])
                t_hi = (yield from act.go(lambda e: e.activation(q[:, :, :, 0, :], src, ACT.Copy), t_in, qfree, cost=0.31))
                t_lo = (yield from pool.go(lambda e: e.tensor_tensor(
                    q[:, :, :, 1, :], src, q[:, :, :, 0, :].bitcast(F32), ALU.subtract), t_hi, cost=0.7))
                wu, wfree = yield from wus.take()
                t_wu = (yield from pool.go(lambda e: e.tensor_tensor(
                    wu[:], b4[:, k, :].unsqueeze(1).broadcast_to([P, 32, NS]),
                    w["wu_mask"][:].unsqueeze(2).broadcast_to([P, 32, NS]), ALU.mult),
                    wfree, t_in, ld("wu_mask"), cost=1.0))
                bank, bfree = yield from gen.take()
                t = (yield from mms([(bank[:, blk(c)], [(q[:, c].rearrange("p a b r -> p (a b r)"), ident_r[:])])
                         for c in range(IC)], bfree, t_hi, t_lo, t_identr))
                xqs.give(q, t)
                row, rfree = yield from xrows.take()
                t_row = (yield from act.go(lambda e: e.activation(row[:], bank[:], ACT.Copy), t, rfree))
                gen.give(bank, t_row)
                laid_out.append((row, t_row, wu, t_wu, [t_hi, t_lo]))
            handed["laid out", g] = t_wu

        def bring_in(g):
            for k in range(NX):
                while not laid_out:
                    yield WAIT
                row, t_row, wu, t_wu, t_read = laid_out.pop(0)
                for s in range(STEPS_X):
                    u, free = yield from us.take()
                    t = (yield from mm(u[:], [(wu[:].rearrange("p m n -> p (m n)")[:, blk(s)], row[:])],
                              t_row, t_wu, free))
                    brought.append((u, t, t_read))
                xrows.give(row, t)
                wus.give(wu, t)

        def scan(g):
            while ("scan inputs", g) not in handed:
                yield WAIT
            (X, decay, c_rows, b4), t_in = handed["scan inputs", g]
            h, free = yield from hs.take()
            t_h = (yield from dve.go(lambda e: e.memset(h[:], 0.0), free, cost=0.3))
            start = h
            for step in range(T):
                while not brought:
                    yield WAIT
                u, t_u, t_read = brought.pop(0)
                last, (h, free) = h, (yield from hs.take())
                t_p = (yield from dve.go(lambda e: e.scalar_tensor_tensor(
                    h[:], last[:], decay[:, step:step + 1], u[:], ALU.mult, ALU.add), t_u, t_h, free, t_in, cost=0.66))
                us.give(u, t_p)
                if step == 0:
                    hs.give(start, t_p)
                t_h = (yield from dve.go(lambda e: e.tensor_scalar(
                    h[:], h[:], CLIP, -CLIP, ALU.min, ALU.max), t_p, cost=0.34))
                stepped.append((h, t_h, t_read))
            handed["stepped", g] = t_h

        def read_out(g):
            while ("scan inputs", g) not in handed:
                yield WAIT
            inputs, t_in = handed.pop(("scan inputs", g))
            X, decay, c_rows, b4 = inputs
            t_out, t_diags = [], []
            for k16 in range(T // 16):
                cdiag, dfree = yield from cdiags.take()
                t_diag = []
                for q in range(4):
                    t0 = 16 * k16 + 4 * q
                    t_diag.append((yield from dve.go(lambda e: e.tensor_tensor(
                        cdiag[:, 4 * q:4 * q + 4, 8 * q:8 * q + 8],
                        c_rows[:, t0:t0 + 4].unsqueeze(2).broadcast_to([P, 4, GB]),
                        w["c_mask"][:].unsqueeze(1).broadcast_to([P, 4, GB]), ALU.mult),
                        dfree, t_in, t_zero_cd, ld("c_mask"), cost=0.1)))
                t_diags += t_diag
                y, yfree = yield from ys.take()
                for q in range(4):
                    while len(stepped) < STEPS_X:
                        yield WAIT
                    states = [stepped.pop(0) for _ in range(STEPS_X)]

                    def go(e):
                        for j in range(4):
                            last = e.matmul(y[32 * j:32 * j + 32, :], cdiag[:, 4 * q + j, :],
                                            states[j][0][:], start=q == 0, stop=q == 3)
                        return last
                    t = (yield from pe.go(go, [t for _, t, _ in states], t_diag, yfree, cost=1.1))
                    for h, _, _ in states:
                        hs.give(h, t)
                cdiags.give(cdiag, t)
                ytok, tfree = yield from ytoks.take()
                t = (yield from act.go(lambda e: e.activation(ytok[:], y[:], ACT.Copy), t, tfree))
                ys.give(y, t)
                bank, bfree = yield from gen.take()
                t = (yield from transposes([(bank[:, blk(c)], ytok[:, blk(c)]) for c in range(IC)], t, bfree))
                ytoks.give(ytok, t)
                cols16, view = blk(k16), "p (q j b) -> p q j b"
                for c in range(IC):
                    t_d = (yield from act.go(lambda e: e.activation(
                        X[:, c, cols16], X[:, c, cols16], ACT.Copy, scale=w["vecs"][:, 3, c:c + 1]),
                        states[-1][2], t_in, cost=0.3))
                    t_out.append((yield from dve.go(lambda e: e.tensor_tensor(
                        X[:, c, cols16].rearrange(view, q=4, b=GB), X[:, c, cols16].rearrange(view, q=4, b=GB),
                        bank[:, blk(c)].rearrange("p (j q b) -> p q j b", q=4, b=GB), ALU.add), t_d, t,
                        cost=0.2)))
                gen.give(bank, t_out[-IC:])
            handed["scan", g] = (inputs, t_out, [handed.pop(("laid out", g)), handed.pop(("stepped", g)), t_diags])

        arrived = []

        def expert_weights(g):
            for name, (parts, n) in EXPERT_SHAPES.items():
                per = min(parts, WSLOT // n)
                for p0 in range(0, parts, per):
                    buf, free = yield from wring.take()
                    nbuf = wring_index[id(buf)]
                    landed[nbuf] += 16
                    view = buf[:, 0:per * n].rearrange("p (c n) -> p c n", n=n)
                    yield sp, max([sp.sees(t) for t in free], default=0.0), None
                    t = sp.dma(sem(f"wring{nbuf}"), landed[nbuf],
                               lambda e: e.dma_start(view, dram[name][:, p0:p0 + per, :]), free)
                    arrived.append((name, buf, view, t))

        landed = [0] * WRING
        wring_index = {id(b): i for i, (b, _) in enumerate(wring.bufs)}

        def weight_of(name):
            parts, n = EXPERT_SHAPES[name]
            chunks, ticks, bufs = [], [], []
            while len(chunks) < parts:
                while not arrived:
                    yield WAIT
                got, buf, view, t = arrived.pop(0)
                assert got == name, "weights arrive in the order of their use"
                chunks += [view[:, i, :] for i in range(view.shape[1])]
                ticks.append(t)
                bufs.append(buf)
            return chunks, ticks, bufs

        def drop_weight(bufs, t):
            for b in bufs:
                wring.give(b, t)

        def dense(pool_, xs, weight, chunks, func, last_use=False):
            res = []
            wc, t_w, bufs = yield from weight_of(weight)
            cuts = [range(0, len(xs) - 1), range(len(xs) - 1, len(xs))]
            for m0 in range(0, chunks, 2):
                out = {}
                for m in (m0, m0 + 1):
                    out[m] = yield from gen.take()
                for cs in cuts:
                    for m, (bank, free) in out.items():
                        t = yield from accumulate(bank[:], [(wc[c][:, blk(m)], xs[c][0][:]) for c in cs],
                                                  cs is cuts[0], cs is cuts[1], free, [xs[c][1] for c in cs], t_w)
                        if cs is cuts[0]:
                            continue
                        if last_use and m == chunks - 1:
                            drop(pool_, xs, t)
                        tile, tfree = yield from pool_.take()
                        t_f = (yield from act.go(lambda e: e.activation(tile[:], bank[:], func), t, tfree, table=TABLE[func]))
                        gen.give(bank, t_f)
                        res.append((tile, t_f))
            drop_weight(bufs, t)
            return res, t

        def drop(pool_, xs, t):
            for x, _ in xs:
                pool_.give(x, t)

        def rms_norm(tiles, xs, which):
            bank, t = yield from token_sums(tiles, [(x[:], t) for x, t in xs], col_rms)
            r, t = yield from rsqrt_of(bank, t, EPS_RMS)
            bank, t = yield from over_tokens(r[:, 8:8 + BLK], t)
            small.give(r, t)
            res = []
            for kc, (x, t_x) in enumerate(xs):
                tile, free = (yield from tiles.take())
                res.append((tile, (yield from dve.go(lambda e, o=tile, x=x, kc=kc: e.scalar_tensor_tensor(
                    o[:], x[:], w["norms"][:, kc, which:which + 1], bank[:], ALU.mult, ALU.mult),
                    free, t, t_x, ld("norms")))))
            gen.give(bank, [t for _, t in res])
            return res

        def attention(tiles, h, blocks):
            ao_t = [[], []]
            for bp in blocks:
                qk, free = (yield from gen.take())
                ht = [t for _, t in h]
                t_qk = (yield from mm(qk[:], [(h[kc][0][:, blk(bp)], w["w_qk"][:, kc, :]) for kc in range(KC)],
                          free, ht, ld("w_qk")))
                vb, free = (yield from gen.take())
                t_v = (yield from mms([(vb[64 * par:64 * par + 64, P * b:P * b + P],
                            [(h[kc][0][:, P * bp + T * b:P * bp + T * b + T],
                              w["w_v"][:, kc, :].rearrange("p (h two d) -> p two h d", two=2, d=HD)[:, par])
                             for kc in range(KC)]) for b in range(2) for par in range(2)],
                          free, ld("w_v")))
                vd, vfree = (yield from vbd.take())
                t_vd = []
                for par in range(2):
                    t_vd.append((yield from act.go(lambda e: e.activation(
                        vd[64 * par:64 * par + 64, :, :, HD * par:HD * par + HD].rearrange("p b h d -> p (b h) d"),
                        vb[64 * par:64 * par + 64, 0:256].rearrange("p (x d) -> p x d", d=HD), ACT.Copy),
                        t_v, vfree, t_zero_v, cost=0.27)))
                gen.give(vb, t_vd)
                sq, free = (yield from tiles.take())
                t = (yield from act.go(lambda e: e.activation(sq[:], qk[:], ACT.Square), t_qk, free))
                ss, sfree = (yield from small.take())
                t = (yield from dve.go(lambda e: e.tensor_reduce(
                    ss[:, 0:32], sq[:].rearrange("p (h d) -> p h d", d=HD), AX, ALU.add), t, sfree))
                tiles.give(sq, t)
                t = (yield from dve.go(lambda e: e.tensor_scalar(ss[:, 0:32], ss[:, 0:32], 1.0 / HD, EPS_RMS,
                                                     ALU.mult, ALU.add), t, cost=TINY))
                t = (yield from pool.go(lambda e: e.tensor_tensor(
                    ss[:, 32:64], ss[:, 0:32], neg_half.broadcast_to([P, 32]), ALU.pow), t, ld("cols"), cost=5.6))
                qkn, free = (yield from tiles.take())
                t = (yield from dve.go(lambda e: e.tensor_tensor(
                    qkn[:].rearrange("p (h d) -> p h d", d=HD), qk[:].rearrange("p (h d) -> p h d", d=HD),
                    ss[:, 32:64].unsqueeze(2).broadcast_to([P, 32, HD]), ALU.mult), t, free))
                gen.give(qk, t)
                small.give(ss, t)
                bank, free = (yield from gen.take())
                t = (yield from transposes([(bank[:, blk(i)], qkn[:, blk(i)]) for i in range(4)], t, free))
                tiles.give(qkn, t)
                qkt, free = (yield from tiles.take())
                t_qt = []
                for i in range(2):
                    t_qt.append((yield from act.go(lambda e: e.activation(
                        qkt[:, 256 * i:256 * i + 256], bank[:, 256 * i:256 * i + 256], ACT.Copy,
                        scale=w["qkn"][:, i:i + 1]), t, free, ld("qkn"), cost=0.36)))
                gen.give(bank, t_qt)
                scores, t_s = [], []
                for c in range(KC):
                    kd = []
                    for b in range(2):
                        kbd, free = (yield from tiles.take())
                        kd.append((kbd, (yield from pool.go(lambda e, o=kbd, c=c, b=b: e.tensor_tensor(
                            o[:].rearrange("p (h k) -> p h k", k=T),
                            qkt[:, 256 + P * c + T * b:256 + P * c + T * b + T].unsqueeze(1).broadcast_to([P, 8, T]),
                            w["head_mask"][:].unsqueeze(2).broadcast_to([P, 8, T]), ALU.mult),
                            t_qt, free, ld("head_mask"), cost=1.0))))
                    bank, free = (yield from gen.take())
                    t = (yield from mms([(bank[T * b:T * b + T, :],
                              [(qkt[:, P * c + T * b:P * c + T * b + T], kd[b][0][:])]) for b in range(2)],
                            free, t_qt, [t for _, t in kd]))
                    for x, _ in kd:
                        tiles.give(x, t)
                    sc, free = (yield from tiles.take())
                    scv = sc[:].rearrange("p (h k) -> p h k", k=T)
                    t_m = (yield from dve.go(lambda e, i=bank, o=scv: e.scalar_tensor_tensor(
                        o, i[:].rearrange("p (h k) -> p h k", k=T), HD ** -0.5,
                        w["causal"][:].unsqueeze(1).broadcast_to([P, 8, T]), ALU.mult, ALU.add),
                        t, free, ld("causal")))
                    gen.give(bank, t_m)
                    scores.append((sc, scv, t_m))
                    t_s.append(t)
                tiles.give(qkt, t_s)
                st, sfree = (yield from small.take())
                probs = []
                for c, (sc, scv, t) in enumerate(scores):
                    m = st[:, 8 * c:8 * c + 8]
                    t = (yield from dve.go(lambda e, m=m, i=scv: e.tensor_reduce(m, i, AX, ALU.max), t, sfree))
                    t = (yield from pool.go(lambda e, m=m, i=scv: e.tensor_tensor(
                        i, i, m.unsqueeze(2).broadcast_to([P, 8, T]), ALU.subtract), t, cost=1.0))
                    t = (yield from act.go(lambda e, i=sc: e.activation(i[:], i[:], ACT.Exp), t, table="exp"))
                    bank, free = (yield from gen.take())
                    t = (yield from transposes([(bank[:, blk(i)], sc[:, blk(i)]) for i in range(4)], t, free))
                    tiles.give(sc, t)
                    pt, free = (yield from tiles.take())
                    t_p = (yield from act.go(lambda e, o=pt, i=bank: e.activation(o[:], i[:], ACT.Copy), t, free))
                    gen.give(bank, t_p)
                    probs.append((pt, t_p))
                ob, free = (yield from gen.take())
                t = (yield from mms([(ob[T * b:T * b + T, VW * hp:VW * hp + VW],
                          [(probs[hp // 4][0][:, P * (hp % 4) + T * b:P * (hp % 4) + T * b + T],
                            vd[:, b, hp])])
                         for hp in range(8) for b in range(2)], free, [t for _, t in probs], t_vd))
                vbd.give(vd, t)
                for x, _ in probs:
                    tiles.give(x, t)
                out_v = ob[:, 0:VW * HEADS // 2].rearrange("p (h w) -> p h w", w=VW)
                t_r = (yield from dve.go(lambda e: e.reciprocal(
                    st[:, 32:48].rearrange("p (h two) -> p h two", two=2), out_v[:, :, 2 * HD:VW]), t, cost=0.17))
                on, free = (yield from tiles.take())
                t = (yield from dve.go(lambda e: e.tensor_tensor(
                    on[:, 0:C].rearrange("p (h two d) -> p h two d", two=2, d=HD),
                    out_v[:, :, 0:2 * HD].rearrange("p h (two d) -> p h two d", d=HD),
                    st[:, 32:48].rearrange("p (h two) -> p h two", two=2).unsqueeze(3).broadcast_to(
                        [P, HEADS // 2, 2, HD]), ALU.mult), t_r, free, cost=0.34))
                gen.give(ob, t)
                small.give(st, t)
                bank, free = (yield from gen.take())
                t = (yield from transposes([(bank[:, blk(i)], on[:, blk(i)]) for i in range(KC)], t, free))
                tiles.give(on, t)
                for kc in range(KC):
                    ao_t[kc].append((yield from act.go(lambda e, kc=kc, bp=bp: e.activation(
                        h[kc][0][:, blk(bp)], bank[:, blk(kc)], ACT.Copy), t, t_qk, t_v, cost=0.16)))
                gen.give(bank, ao_t[0][-1], ao_t[1][-1])
            return ao_t

        def attention_half(g):
            while ("h", g) not in handed:
                yield WAIT
            handed["attended", g] = yield from attention(half_tiles, handed.pop(("h", g)), range(BLK // 2, BLK))

        def gate(xf):
            bank, free = (yield from gen.take())
            t = (yield from mms([(bank[:, i * EXPERTS:(i + 1) * EXPERTS],
                      [(xf[kc][0][:, blk(i)], w["w_gate"][:, kc, :]) for kc in range(KC)])
                     for i in range(BLK)], free, [t for _, t in xf], ld("w_gate")))
            return bank, t

        def top_two(bank, t):
            nb = BLK * EXPERTS
            a, afree = (yield from small.take())
            d, dfree = (yield from small.take())
            f, ffree = (yield from small.take())
            pr, st, wt = a[:, 0:nb], a[:, 16:20], a[:, 32:32 + nb]

            def v(ap):
                return ap.rearrange("p (i e) -> p i e", e=EXPERTS)

            def per(ap):
                return ap.unsqueeze(2).broadcast_to([P, BLK, EXPERTS])
            t = (yield from dve.go(lambda e: e.tensor_scalar(pr, bank[:, 0:nb], FMAX, -FMAX, ALU.min, ALU.max), t, afree, cost=TINY))
            gen.give(bank, t)
            t = (yield from dve.go(lambda e: e.tensor_reduce(st, v(pr), AX, ALU.max), t, cost=TINY))
            t = (yield from dve.go(lambda e: e.tensor_tensor(v(pr), v(pr), per(st), ALU.subtract), t, cost=TINY))
            t = (yield from act.go(lambda e: e.activation(pr, pr, ACT.Exp), t, cost=0.2, table="exp"))
            t = (yield from dve.go(lambda e: e.tensor_reduce(st, v(pr), AX, ALU.add), t, cost=TINY))
            t = (yield from dve.go(lambda e: e.reciprocal(st, st), t, cost=TINY))
            t = (yield from dve.go(lambda e: e.tensor_tensor(v(pr), v(pr), per(st), ALU.mult), t, cost=TINY))
            t_before = []
            for dst, free, op, which in ((d, dfree, ALU.is_ge, 0), (f, ffree, ALU.is_gt, 1)):
                for i in range(BLK):
                    one = pr[:, 4 * i:4 * i + 4]
                    t2 = (yield from dve.go(lambda e, dst=dst, i=i, one=one, op=op: e.tensor_tensor(
                        v(dst[:, 16 * i:16 * i + 16]), one.unsqueeze(1).broadcast_to([P, 4, 4]),
                        one.unsqueeze(2).broadcast_to([P, 4, 4]), op), t, free, cost=TINY))
                    t_before.append(t2)
                t2 = (yield from dve.go(lambda e, dst=dst, which=which: e.tensor_tensor(
                    dst[:].rearrange("p (i m) -> p i m", m=16), dst[:].rearrange("p (i m) -> p i m", m=16),
                    w["rank"][:, which, :].unsqueeze(1).broadcast_to([P, BLK, 16]), ALU.mult),
                    t_before[-BLK:], ld("rank"), cost=TINY))
                t_before.append(t2)
            t2 = (yield from dve.go(lambda e: e.tensor_tensor(d[:], d[:], f[:], ALU.add), t_before, cost=TINY))
            small.give(f, t2)
            t2 = (yield from dve.go(lambda e: e.tensor_reduce(wt, d[:].rearrange("p (m j) -> p m j", j=4), AX, ALU.add), t2, cost=TINY))
            small.give(d, t2)
            t = (yield from dve.go(lambda e: e.scalar_tensor_tensor(wt, wt, TOPK - 0.5, pr, ALU.is_lt, ALU.mult), t2, cost=TINY))
            t = (yield from dve.go(lambda e: e.tensor_reduce(st, v(wt), AX, ALU.add), t, cost=TINY))
            t = (yield from dve.go(lambda e: e.tensor_scalar(st, st, EPS_TOP, None, ALU.add), t, cost=TINY))
            t = (yield from dve.go(lambda e: e.reciprocal(st, st), t, cost=TINY))
            t = (yield from dve.go(lambda e: e.tensor_tensor(v(wt), v(wt), per(st), ALU.mult), t, cost=TINY))
            return a, wt, t

        def middle(g):
            while ("scan", g) not in handed:
                yield WAIT
            inputs, t_scan, t_coef = handed.pop(("scan", g))
            X, tiles = inputs[0], mid_tiles[g % MIDS]
            xt = yield from load_x(g, "mid", tiles)
            t_z = []
            for c in range(IC):
                bank, free = (yield from gen.take())
                t = (yield from mm(bank[:], [(w["w_z"][:, kc, blk(c)], xt[kc][0][:]) for kc in range(KC)],
                       free, [t for _, t in xt], ld("w_z")))
                sg, sfree = (yield from tiles.take())
                t_sg = (yield from act.go(lambda e: e.activation(sg[:], bank[:], ACT.Silu), t, sfree, table="silu"))
                gen.give(bank, t_sg)
                t_z.append((yield from pool.go(lambda e, c=c, i=sg: e.tensor_tensor(X[:, c, :], X[:, c, :], i[:], ALU.mult),
                                   t_sg, t_scan, cost=1.3)))
                tiles.give(sg, t_z[-1])
            for tile, _ in xt:
                tiles.give(tile, t)
            x1 = []
            for m in range(KC):
                bank, free = (yield from gen.take())
                t = yield from accumulate(bank[:], [(w["w_out"][:, c, blk(m)], X[:, c, :]) for c in range(IC)],
                                          True, True, free, t_z, ld("w_out"))
                tile, tfree = (yield from tiles.take())
                t_x = (yield from act.go(lambda e, o=tile, i=bank: e.activation(
                    o[:].rearrange("p (b t) -> p t b", t=T), t_major(i[:]), ACT.Copy), t, tfree))
                gen.give(bank, t_x)
                x1.append((tile, t_x))
            scan_inputs.give(inputs, t, t_coef)
            h = yield from rms_norm(tiles, x1, 0)
            handed["h", g] = h
            ao_t = yield from attention(tiles, h, range(BLK // 2))
            while ("attended", g) not in handed:
                yield WAIT
            ao = [(h[kc][0], ts) for kc, ts in enumerate(zip(ao_t, handed.pop(("attended", g))))]
            for m in range(KC):
                bank, free = (yield from gen.take())
                lo = KEPT if m == 0 else 0
                t = (yield from mm(bank[lo:, :], [(w["w_o"][:, kc, P * m + lo:P * m + P], ao[kc][0][:]) for kc in range(KC)],
                       free, [t for _, t in ao], ld("w_o")))
                t_x = (yield from dve.go(lambda e, o=x1[m][0], i=bank, lo=lo: e.tensor_tensor(
                    o[lo:, :], o[lo:, :], i[lo:, :], ALU.add), t, x1[m][1], [t for _, t in h]))
                gen.give(bank, t_x)
                x1[m] = (x1[m][0], [t_x, x1[m][1]])
            for tile, _ in ao:
                tiles.give(tile, t)
            xf = yield from rms_norm(tiles, x1, 1)
            acc, free_acc = yield from accs.take()
            t_acc = [sp.dma(sem(f"ld_acc{g}"), 16, lambda e: e.dma_start(
                acc[:], dram["x"][g * TOK:(g + 1) * TOK, :].rearrange("(i p) c -> p i c", p=P)), free_acc)]
            for i2 in range(2):
                bank, free = (yield from gen.take())
                t = (yield from transposes([(bank[:, P * (2 * j + kc):P * (2 * j + kc) + P], x1[kc][0][:, blk(2 * i2 + j)])
                                for j in range(2) for kc in range(KC)], free, x1[0][1], x1[1][1]))
                t_a = (yield from dve.go(lambda e, i2=i2, i=bank: e.tensor_tensor(
                    acc[:, 2 * i2:2 * i2 + 2, :], acc[:, 2 * i2:2 * i2 + 2, :],
                    i[:].rearrange("p (i c) -> p i c", c=C), ALU.add), t, t_acc[0]))
                gen.give(bank, t_a)
                t_acc.append(t_a)
            for tile, _ in x1:
                tiles.give(tile, t, [t for _, t in xf])
            logits, t_gate = yield from gate(xf)
            route, wt, t_wt = yield from top_two(logits, t_gate)
            handed["middle", g] = (xf, acc, [t_acc[1], t_acc[1], t_acc[2], t_acc[2]], route, wt, t_wt)

        def experts(g):
            while ("middle", g) not in handed:
                yield WAIT
            xf, acc, last_add, route, wt, t_wt = handed.pop(("middle", g))
            take = hidden_tiles

            def expert(index, hidden, weight):
                wc, t_w, bufs = yield from weight_of(weight)
                for i2 in range(2):
                    bank, free = (yield from gen.take())
                    t = (yield from mms([(bank[:, MOD * j:MOD * j + MOD],
                              [(x[:, blk(2 * i2 + j)], wc[c]) for c, (x, _) in enumerate(hidden)])
                             for j in range(2)], free, [t for _, t in hidden], t_w))
                    t_a = []
                    for j in range(2):
                        i = 2 * i2 + j
                        last_add[i] = (yield from dve.go(lambda e, i=i, j=j, ps=bank: e.scalar_tensor_tensor(
                            acc[:, i, KEPT:], ps[:, MOD * j:MOD * j + MOD],
                            wt[:, EXPERTS * i + index:EXPERTS * i + index + 1], acc[:, i, KEPT:],
                            ALU.mult, ALU.add), t, t_wt, last_add[i], cost=0.33))
                        t_a.append(last_add[i])
                    gen.give(bank, t_a)
                drop(take, hidden, t)
                drop_weight(bufs, t)

            hid, t = yield from dense(take, xf, "e1_w1", IC, ACT.Silu)
            gated = []
            wc, t_w, bufs = yield from weight_of("e1_w2")
            for m in range(IC):
                bank, free = (yield from gen.take())
                t_m = (yield from mm(bank[:], [(wc[kc][:, blk(m)], xf[kc][0][:]) for kc in range(KC)],
                                     free, t_w, [t for _, t in xf]))
                x, t_x = hid[m]
                t = (yield from dve.go(lambda e: e.tensor_tensor(x[:], x[:], bank[:], ALU.mult), t_m, t_x))
                gen.give(bank, t)
                gated.append((x, t))
            drop_weight(bufs, t_m)
            two, t = yield from dense(take, xf, "e2_l1", IC, ACT.Gelu)
            yield from expert(1, gated, "e1_down")
            two, t = yield from dense(take, two, "e2_l2", IC, ACT.Gelu, last_use=True)
            two, t = yield from dense(take, two, "e2_l3", IC, ACT.Gelu, last_use=True)
            zero, t = yield from dense(take, xf, "e0_up", IC, ACT.Gelu)
            yield from expert(2, two, "e2_l4")
            three, t = yield from dense(take, xf, "e3_down", KC, ACT.Gelu)
            drop(mid_tiles[g % MIDS], xf, t)
            yield from expert(0, zero, "e0_down")
            three, t = yield from dense(take, three, "e3_up", IC, ACT.Gelu, last_use=True)
            yield from expert(3, three, "e3_out")
            small.give(route, last_add)
            accs.give(acc, sp.dma(sem(f"stores{g % 2}"), 16 * (g // 2 + 1), lambda e: e.dma_start(
                out[g * TOK:(g + 1) * TOK, :].rearrange("(i p) c -> p i c", p=P), acc[:]), last_add))

        class Stage:

            def __init__(self, name, steps, eager=EAGER, first=EAGER_FIRST, groups=range(GROUPS)):
                self.name, self.eager, self.first, self.coming = name, eager, first, (sp, 0.0, None)
                self.group = groups[0]
                self.run = self.every_group(steps, groups)

            def every_group(self, steps, groups):
                for self.group in groups:
                    yield from steps(self.group)

            def start(self):
                lane, due, table = self.coming
                head_start = self.eager + self.first * max(0, FIRST - self.group) / FIRST
                return max(lane.clock, due) + lane.switch(table) - head_start

            def go_on(self):
                for lane in lanes:
                    lane.phase(f"{self.name}{self.group // 2}")
                self.coming = next(self.run, None)

        stages = [Stage("w", expert_weights, 0.0), Stage("scan", scan), Stage("bring", bring_in),
                  Stage("read", read_out), Stage("lay", lay_out), Stage("front", front, 0.0),
                  *[Stage(f"mid{j}_", middle, groups=range(j, GROUPS, MIDS)) for j in range(MIDS)],
                  Stage("half", attention_half), Stage("exp", experts, 0.0, first=0.0)]
        while stages:
            due = sorted((s for s in stages if s.coming != WAIT), key=Stage.start)
            blocked = [s for s in stages if s.coming == WAIT]
            moved = False
            for stage in blocked + due[:1]:
                was = stage.coming
                stage.go_on()
                moved = moved or stage.coming != WAIT or was != WAIT
            stages = [s for s in stages if s.coming is not None]
            assert moved, "the stages wait for one another"

        for half in range(2):
            sp.wait(Tick(sem(f"stores{half}"), 16 * GROUPS // 2, 0.0))


def chunked(a, parts):
    return np.ascontiguousarray(a.reshape(parts, P, -1).transpose(1, 0, 2))


def lay_weights(v):
    c, f = (lambda n: v["L0_cond_" + n]), (lambda n: v["L0_ffn_" + n])
    d = {}
    d["w_xr"], d["w_z"] = (chunked(half, KC) for half in np.split(c("W_in").T, 2, axis=1))
    wx = c("W_xproj").T
    gap = np.zeros((DI, NS), wx.dtype)
    d["w_x"] = chunked(np.concatenate([wx[:, NS:2 * NS], gap, wx[:, 2 * NS:], gap, wx[:, 0:NS]], 1), IC)
    d["w_out"] = chunked(c("W_out").T, IC)
    d["w_qk"] = chunked(np.concatenate([f("wq").T, f("wk").T], 1), KC)
    for name, key, n in (("w_v", "wv", KC), ("w_o", "wo", KC), ("w_gate", "gate_w", KC), ("e0_up", "e0_up", KC),
                         ("e1_w1", "e1_w1", KC), ("e1_w2", "e1_w2", KC), ("e2_l1", "e2_l1", KC),
                         ("e2_l2", "e2_l2", IC), ("e2_l3", "e2_l3", IC), ("e3_down", "e3_down", KC),
                         ("e3_up", "e3_up", KC)):
        d[name] = chunked(f(key).T, n)
    for name in ("e0_down", "e1_down", "e2_l4", "e3_out"):
        d[name] = chunked(f(name).T[:, KEPT:], IC)
    d["temb"] = chunked(v["cond_2048"].T, IC)
    d["w_conv"] = chunked(c("W_conv").reshape(DI, NCONV), IC)
    d["vecs"] = np.ascontiguousarray(np.stack(
        [c(n).reshape(IC, P).T for n in ("b_conv", "ln_g", "ln_b", "D")], 1))
    d["norms"] = np.ascontiguousarray(np.stack([f(n).reshape(KC, P).T for n in ("n1_w", "n2_w")], 2))
    d["qkn"] = np.ascontiguousarray(np.stack([np.tile(f(n), P // HD) for n in ("qn_w", "kn_w")], 1))
    dt_w = np.zeros((P, NS + 2), wx.dtype)
    dt_w[32:48, 0:NS] = c("W_dt").T
    dt_w[32:48, NS] = c("b_dt")
    dt_w[32:48, NS + 1] = c("A_log")
    d["dt_w"] = dt_w
    return d


def lay_constants():
    d, i = {}, np.arange(P)
    d["ident"] = np.eye(P)
    d["sel"] = (i[:, None, None] == 32 * np.arange(BLK)[None, :, None] + (i % 32)[None, None, :])
    d["mean_mat"] = np.full((P, P), 1.0 / DI)
    d["cols"] = np.tile([1.0 / DI, 1.0 / C, 1.0, -0.5, 0.5], (P, 1))
    d["wu_mask"] = (i % 32)[:, None] == np.arange(32)[None, :]
    d["c_mask"] = (i // NS)[:, None] == np.arange(GB)[None, :]
    d["causal"] = np.where(np.arange(T)[None, :] <= (i % T)[:, None], 0.0, MASKED)
    d["head_mask"] = (i // HD)[:, None] == np.arange(8)[None, :]
    e = np.arange(EXPERTS)
    lower = (e[None, :] < e[:, None]).reshape(-1)
    upper = (e[None, :] > e[:, None]).reshape(-1)
    d["rank"] = np.tile(np.stack([lower, upper])[None], (P, 1, 1))
    return {k: np.ascontiguousarray(a.astype(np.float32)) for k, a in d.items()}


def kernel(**inputs):
    import concourse.bacc as bacc
    from concourse.bass_utils import run_bass_kernel_spmd

    v = {k: np.asarray(a) for k, a in inputs.items()}
    arrays = {**lay_weights(v), **lay_constants()}
    x = v["x"]
    arrays["xT"] = np.ascontiguousarray(
        x.reshape(GROUPS, GB, T, KC, P).transpose(3, 4, 0, 2, 1).reshape(KC, P, GROUPS, TOK))
    arrays["x"] = np.ascontiguousarray(x.reshape(B * T, C))
    for k, s in {**W_SHAPES, **EXPERT_SHAPES}.items():
        assert arrays[k].shape == (P,) + s, (k, arrays[k].shape)

    nc = bacc.Bacc("TRN2", target_bir_lowering=False, num_devices=1)
    dram = {k: nc.dram_tensor(f"in_{k}", a.shape, mybir.dt.from_np(a.dtype), kind="ExternalInput").ap()
            for k, a in arrays.items()}
    out = nc.dram_tensor("out_y", (B * T, C), F32, kind="ExternalOutput").ap()
    build_program(nc, dram, out)
    r = run_bass_kernel_spmd(nc, [{f"in_{k}": a for k, a in arrays.items()}], core_ids=[0])
    return r.results[0]["out_y"].reshape(B, T, C)
```
